# Optimizing a Trainium2 kernel written in Bass

```python
import numpy as np
import jax
import jax.numpy as jnp

def _softmax(x, axis=-1):
    return jax.nn.softmax(x, axis=axis)

def _gelu(x):
    return jax.nn.gelu(x, approximate=True)

def _silu(x):
    return jax.nn.silu(x)

def _sigmoid(x):
    return jax.nn.sigmoid(x)

def _layernorm(x, axis=-1, eps=1e-05):
    m = jnp.mean(x, axis=axis, keepdims=True)
    v = jnp.var(x, axis=axis, keepdims=True)
    return (x - m) / jnp.sqrt(v + eps)

def _scatter_add(tgt, idx, src, axis=0):
    return tgt.at[idx].add(src)

def _segment_sum(src, seg, n):
    return jax.ops.segment_sum(src, seg, n)
kernel_name = 'mk_adj_preln_d4_adj_r2_d72817'

def setup_inputs(seed: int=0):
    np.random.seed(seed)
    _w = jnp.asarray

    def _rec_inputs():
        import jax
        import jax.numpy as jnp
        _gk = jax.random.key(seed)
        x = -0.000929 + 1 * jax.random.normal(jax.random.fold_in(_gk, 1), (8192, 128), jnp.float32)
        _w = (1.0 + jnp.arange(8192, dtype=jnp.float32)) ** (-0.5)
        _w = _w / _w.mean()
        _pij = jnp.clip(0.000488281 * _w[:, None] * _w[None, :], 0.0, 1.0)
        _a = jax.random.uniform(jax.random.fold_in(_gk, 2), (8192, 8192)) < _pij
        adj = _a.astype(jnp.int32)
        return (x, adj)
    x, adj = _rec_inputs()

    def _L0_gnn_setup():
        import jax, jax.numpy as jnp
        import numpy as np
        NEG_INF = -9000000000000000.0
        ALPHA = 0.2
        key = jax.random.key(seed)
        k1, k2, k3, k4 = jax.random.split(key, 4)
        N, F_in, F_out = (4096, 128, 128)
        x = jax.random.normal(k1, (N, F_in), dtype=jnp.float32)
        adj = jax.random.randint(k2, (N, N), 0, 2, dtype=jnp.int32)
        W = jax.random.normal(k3, (F_in, F_out), dtype=jnp.float32) * (1.0 / np.sqrt(F_in))
        a = jax.random.normal(k4, (2 * F_out, 1), dtype=jnp.float32) * (1.0 / np.sqrt(2 * F_out))
        return {'x': x, 'adj': adj, 'W': W, 'a': a}
    _L0_gnn_all = _L0_gnn_setup()
    _L0_gnn_in = {k: v for k, v in _L0_gnn_all.items() if k in ('W', 'a')}
    del _L0_gnn_all

    def _L1_gnn_setup():
        import jax, jax.numpy as jnp
        import numpy as np
        NEG_INF = -9000000000000000.0
        LEAKY_SLOPE = 0.01
        key = jax.random.key(seed)
        k1, k2, k3, k4 = jax.random.split(key, 4)
        N, F = (4096, 128)
        inp = jax.random.normal(k1, (N, F), dtype=jnp.float32)
        adj = jax.random.randint(k2, (N, N), 0, 2, dtype=jnp.int32)
        gain = 1.414
        limW = gain * np.sqrt(6.0 / (F + F))
        W = jax.random.uniform(k3, (F, F), minval=-limW, maxval=limW, dtype=jnp.float32)
        lima = gain * np.sqrt(6.0 / (2 * F + 1))
        a = jax.random.uniform(k4, (2 * F, 1), minval=-lima, maxval=lima, dtype=jnp.float32)
        return {'input': inp, 'adj': adj, 'W': W, 'a': a}
    _L1_gnn_all = _L1_gnn_setup()
    _L1_gnn_in = {k: v for k, v in _L1_gnn_all.items() if k in ('W', 'a')}
    del _L1_gnn_all

    def _L2_gnn_setup():
        import jax, jax.numpy as jnp
        import numpy as np
        N = 4096
        IN = 128
        OUT = 128
        THR = 0.0001
        ALPHA = 0.2
        NEG = -1000000000.0
        key = jax.random.key(seed)
        k1, k2, k3, k4 = jax.random.split(key, 4)
        inp = jax.random.normal(k1, (N, IN), jnp.float32)
        W = jax.random.normal(k2, (IN, OUT), jnp.float32) * (1.414 * np.sqrt(2.0 / (IN + OUT)))
        a = jax.random.normal(k3, (2 * OUT, 1), jnp.float32) * (1.414 * np.sqrt(2.0 / (2 * OUT + 1)))
        adj = jax.random.randint(k4, (N, N), 0, 2, jnp.int32)
        return {'input': inp, 'W': W, 'a': a, 'adj': adj, 'M': N}
    _L2_gnn_all = _L2_gnn_setup()
    _L2_gnn_in = {k: v for k, v in _L2_gnn_all.items() if k in ('W', 'a')}
    del _L2_gnn_all

    def _L3_gnn_setup():
        import jax, jax.numpy as jnp
        import numpy as np
        NEG_INF = -9000000000000000.0
        ALPHA = 0.2
        key = jax.random.key(seed)
        k1, k2, k3, k4 = jax.random.split(key, 4)
        N, F_IN, H, D = (4096, 128, 4, 32)
        h = jax.random.normal(k1, (N, F_IN), dtype=jnp.float32)
        adj = jax.random.randint(k2, (N, N), 0, 2, dtype=jnp.int32)
        W = jax.random.normal(k3, (F_IN, H * D), dtype=jnp.float32) * (1.0 / np.sqrt(F_IN))
        a = jax.random.normal(k4, (1, H, 2 * D), dtype=jnp.float32)
        return {'h': h, 'adj': adj, 'W': W, 'a': a}
    _L3_gnn_all = _L3_gnn_setup()
    _L3_gnn_in = {k: v for k, v in _L3_gnn_all.items() if k in ('W', 'a')}
    del _L3_gnn_all
    return {'x': x, 'adj': adj, 'L0_gnn_W': _L0_gnn_in['W'], 'L0_gnn_a': _L0_gnn_in['a'], 'L1_gnn_W': _L1_gnn_in['W'], 'L1_gnn_a': _L1_gnn_in['a'], 'L2_gnn_W': _L2_gnn_in['W'], 'L2_gnn_a': _L2_gnn_in['a'], 'L3_gnn_W': _L3_gnn_in['W'], 'L3_gnn_a': _L3_gnn_in['a']}

def reference(x, adj, L0_gnn_W, L0_gnn_a, L1_gnn_W, L1_gnn_a, L2_gnn_W, L2_gnn_a, L3_gnn_W, L3_gnn_a):
    import jax
    import jax.numpy as jnp

    def _L0_gnn_ref(x, adj, W, a):
        import jax, jax.numpy as jnp
        import numpy as np
        NEG_INF = -9000000000000000.0
        ALPHA = 0.2
        h = x @ W
        F_out = h.shape[1]
        a_src = a[:F_out, 0]
        a_dst = a[F_out:, 0]
        s_src = h @ a_src
        s_dst = h @ a_dst
        e = jax.nn.leaky_relu(s_src[:, None] + s_dst[None, :], negative_slope=ALPHA)
        e = jnp.where(adj > 0, e, jnp.float32(NEG_INF))
        attention = jax.nn.softmax(e, axis=1)
        h_prime = attention @ h
        return h_prime

    def _L1_gnn_ref(input, adj, W, a):
        import jax, jax.numpy as jnp
        import numpy as np
        NEG_INF = -9000000000000000.0
        LEAKY_SLOPE = 0.01
        F_ = W.shape[0]
        h = input @ W
        a1, a2 = (a[:F_, 0], a[F_:, 0])
        s1 = h @ a1
        s2 = h @ a2
        e = jax.nn.leaky_relu(s1[:, None] + s2[None, :], negative_slope=LEAKY_SLOPE)
        masked = jnp.where(adj > 0, e, jnp.float32(NEG_INF))
        attention = jax.nn.softmax(masked, axis=1)
        return attention @ h

    def _L2_gnn_ref(input, W, a, adj, M):
        import jax, jax.numpy as jnp
        import numpy as np
        N = 4096
        IN = 128
        OUT = 128
        THR = 0.0001
        ALPHA = 0.2
        NEG = -1000000000.0
        h = input @ W
        a_src = a[:OUT, 0]
        a_dst = a[OUT:, 0]
        e = jax.nn.leaky_relu((h[:M] @ a_src)[:, None] + (h @ a_dst)[None, :], negative_slope=ALPHA)
        valid = (adj[:M] > 0) & (h.sum(axis=1) != 0)[None, :]
        att = jax.nn.softmax(jnp.where(valid, e, NEG), axis=1)
        att = jnp.where(valid, att, 0.0)
        L = valid.sum(axis=1).astype(h.dtype)
        top = att.max(axis=1)
        attention = jnp.where(att >= THR, att, 0.0) * L[:, None]
        attention = jnp.where((top > THR)[:, None], attention, 0.0)
        h_prime = attention @ h
        return jax.nn.elu(h[:M] + h_prime)

    def _L3_gnn_ref(h, adj, W, a):
        import jax, jax.numpy as jnp
        import numpy as np
        NEG_INF = -9000000000000000.0
        ALPHA = 0.2
        N = h.shape[0]
        H = a.shape[1]
        D = a.shape[2] // 2
        Wh = (h @ W).reshape(N, H, D)
        a_src = a[0, :, :D]
        a_dst = a[0, :, D:]
        s_src = jnp.einsum('nhd,hd->nh', Wh, a_src)
        s_dst = jnp.einsum('nhd,hd->nh', Wh, a_dst)
        e = s_src[:, None, :] + s_dst[None, :, :]
        e = jnp.where(e >= 0, e, ALPHA * e)
        e = jnp.where(adj[:, :, None] > 0, e, NEG_INF)
        attention = jax.nn.softmax(e, axis=1)
        h_prime = jnp.einsum('ijh,jhd->ihd', attention, Wh)
        return jax.nn.elu(h_prime.reshape(N, H * D))
    h = jnp.maximum(_layernorm(x, axis=-1), 0.0)
    x = x + _L0_gnn_ref(h, adj, L0_gnn_W, L0_gnn_a)
    h = jnp.maximum(_layernorm(x, axis=-1), 0.0)
    x = x + _L1_gnn_ref(h, adj, L1_gnn_W, L1_gnn_a)
    h = jnp.maximum(_layernorm(x, axis=-1), 0.0)
    x = x + _L2_gnn_ref(h, L2_gnn_W, L2_gnn_a, adj, 8192)
    h = jnp.maximum(_layernorm(x, axis=-1), 0.0)
    x = x + _L3_gnn_ref(h, adj, L3_gnn_W, L3_gnn_a)
    return x

_drawn_inputs = setup_inputs


def setup_inputs(seed=0):
    import zlib

    import numpy as np

    out = dict(_drawn_inputs(seed))
    spreads = {}
    factors = {}
    for name, (base, spread) in spreads.items():
        noise = np.random.default_rng([zlib.crc32(name.encode()), seed]).standard_normal(out[name].shape)
        drawn = base * np.exp(spread * noise) if base else spread * noise
        out[name] = jnp.asarray(drawn.astype(out[name].dtype))
    for name, factor in factors.items():
        out[name] = (out[name] * factor).astype(out[name].dtype)
    return out
```

```python
from contextlib import ExitStack

import concourse.bass as bass
from concourse import mybir
from concourse.alu_op_type import AluOpType as ALU

FP32 = mybir.dt.float32
BF16 = mybir.dt.bfloat16
I32 = mybir.dt.int32
U32 = mybir.dt.uint32
ACT = mybir.ActivationFunctionType
AX = mybir.AxisListType.X

P = 128
N = 8192
F = 128
TILES = N // P
LAYERS = 4
ALPHA = [0.2, 0.01, 0.2, 0.2]
HEADS = [1, 1, 1, 4]
THRESHOLD = 1e-4
UNIT = float(2.0 ** 83)
LOW = -float(2.0 ** 60)
FLOOR = -3.0e38
EPS = 1e-5
SHIFT = 32
BANK = 4
MAXR = 4


class TileClass:

    def __init__(self, t0, count, runs, rounds, chunks):
        self.t0, self.count, self.runs, self.rounds, self.chunks = t0, count, runs, rounds, chunks
        self.groups = -(-chunks // BANK)
        self.dense = chunks == TILES


class Tile:

    def __init__(self, cls, k, off):
        self.cls, self.k, self.off = cls, k, off
        self.t = k + cls.t0
        self.slot = (cls.t0 + off) % 4
        self.par = self.slot % 2


DENSE0 = TileClass(0, 1, 0, 0, TILES)
SPARSE = [
    DENSE0,
    TileClass(1, 1, 16, 4, 15),
    TileClass(2, 2, 16, 4, 12),
    TileClass(4, 4, 8, 3, 9),
    TileClass(8, 8, 8, 3, 7),
    TileClass(16, 16, 8, 2, 5),
    TileClass(32, 12, 4, 2, 4),
    TileClass(44, 20, 4, 2, 3),
]
DENSE = [TileClass(0, TILES, 0, 0, TILES)]
SLOTS = 15
CHUNKS = sum(c.count * c.chunks for c in SPARSE[1:])


def run_bounds(runs):
    b = [0]
    for i in range(1, runs):
        b.append(max(int(round(N * (i / runs) ** 2 / 32)) * 32, b[-1] + 32))
    return b + [N]


def before(plan, f, tile):
    total = sum(f(c) * c.count for c in plan if c.t0 < tile.cls.t0)
    return total + tile.k * f(tile.cls)


def before_parity(plan, f, tile):
    total = sum(f(c) * c.count for c in plan if c.t0 < tile.cls.t0)
    return (total + tile.off * f(tile.cls)) % 2


def same_slot(plan, f, tile):
    total = sum(f(c) for c in plan if not c.dense and c.t0 < tile.cls.t0
                for k in range(c.count) if (c.t0 + k) % 4 == tile.slot)
    if tile.cls.count < 4:
        return total + f(tile.cls)
    quad = tile.quad
    return total + quad * f(tile.cls) + f(tile.cls)


def same_parity(tile):
    if tile.cls.count < 4:
        return (tile.t + 1) // 2 if tile.par else tile.t // 2
    t = tile.cls.t0 + tile.off
    return tile.quad * 2 + ((t + 1) // 2 if tile.par else t // 2)


def gat_kernel(nc, x, adj, W0, a0, W1, a1, W2, a2, W3, a3, out, force_dense=False):
    Ws, As = [W0, W1, W2, W3], [a0, a1, a2, a3]
    tables = [nc.dram_tensor(f"table{l}", [N, F + HEADS[l]], FP32).ap() for l in range(LAYERS)]
    ctx = ExitStack()
    with ctx:
        def sb(name, shape, dt):
            return ctx.enter_context(nc.sbuf_tensor(name, shape, dt))

        def pb(name, shape, dt=FP32):
            return ctx.enter_context(nc.psum_tensor(name, shape, dt))

        def sem(name):
            return ctx.enter_context(nc.semaphore(name))

        adj_sb = sb("adj_sb", [P, 2 * N], I32)
        ring = adj_sb[:, N:2 * N].bitcast(FP32)
        xs = sb("xs", [P, TILES, F], FP32)
        hs = sb("hs", [P, TILES, F + 8], FP32)
        scores = sb("scores", [P, N], FP32)
        mask = sb("mask", [P, 2, SLOTS * P], BF16)
        onehot = sb("onehot", [P, 2, SHIFT + SLOTS * P], BF16)
        slot_numbers = sb("slot_numbers", [P, SHIFT + SLOTS * P], FP32)
        columns = sb("columns", [P, CHUNKS], U32)
        column_step = sb("column_step", [P, 4, SLOTS], U32)
        attn_t = sb("attn_t", [P, 2, 512], FP32)
        z = sb("z", [P, 4, F], FP32)
        z_t = sb("z_t", [P, 4 * P], FP32)
        wext = sb("wext", [P, LAYERS, F + 8], FP32)
        a_sb = sb("a_sb", [P, LAYERS, 8], FP32)
        ident = sb("ident", [P, P], FP32)
        before_row = sb("before_row", [P, P], FP32)
        mean_of = sb("mean_of", [P, P], FP32)
        zeros = sb("zeros", [P, P], FP32)
        hbar = sb("hbar", [P, F], FP32)
        base = sb("base", [P, 28, 8], FP32)
        first = sb("first", [P, TILES], FP32)
        end = sb("end", [P, TILES], FP32)
        over = sb("over", [P, TILES, 3], FP32)
        top = sb("top", [P, 16, 8], FP32)
        where = sb("where", [P, 16, 8], U32)
        keys = sb("keys", [P, 16, 8], FP32)
        picked = sb("picked", [P, 8 * MAXR], FP32)
        parts = sb("parts", [P, 2, 8 * MAXR, 2], BF16)
        deg = sb("deg", [P, 2], FP32)
        first_step = sb("first_step", [P, 1], FP32)
        listed = sb("listed", [P, SLOTS], FP32)
        over_sum = sb("over_sum", [P, 1], FP32)
        over_int = sb("over_int", [P, 1], I32)
        group_max = sb("group_max", [P, 2, TILES // BANK], FP32)
        st = sb("st", [P, 2, 12, 4], FP32)
        stats = sb("stats", [P, 4, 6], FP32)
        mv = sb("mv", [P, 4, 2], FP32)
        logv = sb("logv", [P, 4], FP32)
        rstd = sb("rstd", [P, 4], FP32)
        eps = sb("eps", [P, 1], FP32)
        row_sum = sb("row_sum", [P, 4], FP32)
        y = sb("y", [P, F], FP32)
        y2 = sb("y2", [P, F], FP32)
        neg = sb("neg", [P, F], FP32)
        exp_neg = sb("exp_neg", [P, F], FP32)

        D = [pb("D0", [P, 512]), pb("D1", [P, 512])]
        PT = [pb("PT0", [P, 512]), pb("PT1", [P, 512])]
        AG = [pb("AG0", [P, F]), pb("AG1", [P, F])]
        HN = PT[0]
        ZT = pb("ZT", [P, 512])
        MEAN = pb("MEAN", [P, F])

        BIGGEST, Q, NEGMAX, SUM, RSUM, VALID, SCALE, EMPTY, COUNT, KEEP = range(10)

        s_w_loaded = sem("s_w_loaded")
        s_x_loaded = sem("s_x_loaded")
        s_consts = sem("s_consts")
        s_base_fill = sem("s_base_fill")
        s_w_t = sem("s_w_t")
        s_w_t_sb = sem("s_w_t_sb")
        s_wa = sem("s_wa")
        s_wext = sem("s_wext")
        s_adj_read = sem("s_adj_read")
        s_tops = sem("s_tops")
        s_keys = sem("s_keys")
        s_picks = sem("s_picks")
        s_deg = sem("s_deg")
        s_parts = sem("s_parts")
        s_row_starts = sem("s_row_starts")
        s_first_step = sem("s_first_step")
        s_onehot = sem("s_onehot")
        s_lists = sem("s_lists")
        s_listed = sem("s_listed")
        s_columns = sem("s_columns")
        s_over = sem("s_over")
        s_over_all = sem("s_over_all")
        s_flag = sem("s_flag")
        s_adj_tile = sem("s_adj_tile")
        s_adj_tile_mask = sem("s_adj_tile_mask")
        s_step_copied = sem("s_step_copied")
        s_mask_half = sem("s_mask_half")
        s_mask = sem("s_mask")
        s_dbcast = sem("s_dbcast")
        s_dscore = sem("s_dscore")
        s_biggest = sem("s_biggest")
        s_q = sem("s_q")
        s_negmax = sem("s_negmax")
        s_scored = sem("s_scored")
        s_leaky = sem("s_leaky")
        s_counted = sem("s_counted")
        s_counted_part = sem("s_counted_part")
        s_exped = sem("s_exped")
        s_normed = sem("s_normed")
        s_attn = sem("s_attn")
        s_pt = sem("s_pt")
        s_pt_sb = sem("s_pt_sb")
        s_agg_group = sem("s_agg_group")
        s_recip = sem("s_recip")
        s_scale = sem("s_scale")
        s_fin_a = sem("s_fin_a")
        s_fin_b = sem("s_fin_b")
        s_fin_y = sem("s_fin_y")
        s_neg = sem("s_neg")
        s_exp_neg = sem("s_exp_neg")
        s_elu = sem("s_elu")
        s_x_done = sem("s_x_done")
        s_bn = sem("s_bn")
        s_mv = sem("s_mv")
        s_logv = sem("s_logv")
        s_rstd = sem("s_rstd")
        s_z = sem("s_z")
        s_zt = sem("s_zt")
        s_z_t = sem("s_z_t")
        s_hn = sem("s_hn")
        s_h_copied = sem("s_h_copied")
        s_hsum = sem("s_hsum")
        s_hs_low = sem("s_hs_low")
        s_h_sb = sem("s_h_sb")
        s_mean_added = sem("s_mean_added")
        s_mean = sem("s_mean")
        s_hbar = sem("s_hbar")
        s_table = sem("s_table")
        s_out = sem("s_out")
        s_adj_loaded = [sem(f"s_adj_loaded{i}") for i in range(2)]
        s_gathered = [sem(f"s_gathered{i}") for i in range(4)]

        block = ctx.enter_context(nc.Block())

        def heads_work(l, plan, tiles):
            units = [(tile, h) for tile in tiles for h in range(HEADS[l])]
            order, waiting = [], None
            for u in units:
                order.append(("F", u))
                if u[0].cls.dense:
                    order.append(("B", u))
                    continue
                if waiting:
                    order.append(("B", waiting))
                waiting = u
            return order + ([("B", waiting)] if waiting else [])

        def layer_units(l):
            return TILES * sum(HEADS[:l])

        def unit_index(l, tile, h):
            return tile.t * HEADS[l] + (layer_units(l) + h)

        def group_base(l, plan):
            return sum(c.count * c.groups for c in plan) * sum(HEADS[:l])

        def group_index(l, plan, tile, h, g):
            return before(plan, lambda c: c.groups, tile) * HEADS[l] + (
                group_base(l, plan) + h * tile.cls.groups + g)

        def group_parity(l, plan, tile, h, g):
            n = before_parity(plan, lambda c: c.groups, tile) * HEADS[l]
            return (n + group_base(l, plan) + h * tile.cls.groups + g) % 2

        def dense_mask_count(l, plan, tile, h, g):
            per_head = TILES // BANK
            per_layer = TILES if plan is DENSE else 1
            return tile.t * (HEADS[l] * per_head) + (per_layer * per_head * sum(HEADS[:l]) + h * per_head + g + 1)

        def bank_free(n, g, tile):
            return n if tile.cls.dense and g == 0 else n - 1

        def unit_parity(l, tile, h):
            return (h if HEADS[l] > 1 else tile.par) % 2 if not tile.cls.dense else 0

        def tile_parity(tile):
            return 0 if tile.cls.dense else tile.par

        def attn_buffer(l, tile, h):
            return scores[:, unit_parity(l, tile, h) * (N // 2):]

        def groups_freed(l, plan, tile, h):
            start = group_index(l, plan, tile, h, 0)
            if tile.cls.dense or (tile.cls.t0 == 1 and h == 0):
                return start
            ahead = tile.cls
            if h == 0 and tile.cls.count < 4 and tile.off == 0:
                ahead = next(c for c in plan if c.t0 <= tile.cls.t0 - 1 < c.t0 + c.count)
            return start - ahead.groups

        def features(l, tile, c, lo, hi):
            if tile.cls.dense:
                return hs[:, c, lo:hi]
            at = tile.slot * SLOTS * (F + 4) + c * (F + HEADS[l])
            return ring[:, at + lo:at + hi]

        def over_plan(eng, plan, body):
            if plan is DENSE:
                body([Tile(plan[0], 0, 0)], None)
                with eng.Fori(1, TILES) as k:
                    body([Tile(plan[0], k, 0)], None)
                return
            body([Tile(c, k, k) for c in plan[:3] for k in range(c.count)], 0)
            for c in plan[3:]:
                if c.count == 4:
                    tiles = [Tile(c, k, k) for k in range(4)]
                    for tile in tiles:
                        tile.quad = 0
                    body(tiles, c.t0 // 4)
                    continue
                with eng.Fori(0, c.count // 4) as quad:
                    tiles = [Tile(c, quad * 4 + k, k) for k in range(4)]
                    for tile in tiles:
                        tile.quad = quad
                    body(tiles, quad + c.t0 // 4)

        def over_quads(eng, body):
            body(0)
            with eng.Fori(1, TILES // 4) as quad:
                body(quad)

        def scan_order(tiles):
            n, order = len(tiles), []
            for i in range(n + 2):
                if i < n:
                    order.append(("A", tiles[i]))
                if 0 <= i - 1 < n:
                    order.append(("B", tiles[i - 1]))
                if 0 <= i - 2 < n:
                    order.append(("C", tiles[i - 2]))
            return order

        def sparse_tiles(eng, body):
            over_plan(eng, SPARSE, lambda tiles, quad: body([t for t in tiles if not t.cls.dense]))

        def due(value):
            return not isinstance(value, int) or value > 0

        @block.sync
        def _(sp):
            for l in range(LAYERS):
                sp.dma_start(wext[:, l, 0:F], Ws[l]).then_inc(s_w_loaded, 16)
            sp.wait_ge(s_consts, 1)
            for l in range(3):
                sp.dma_start(a_sb[:, l, 0:1], As[l][F:2 * F, :]).then_inc(s_w_loaded, 16)
                sp.dma_start(a_sb[:, l, 1:2], As[l][0:F, :]).then_inc(s_w_loaded, 16)
            for h in range(4):
                for side in range(2):
                    sp.dma_start(a_sb[32 * h:32 * h + 32, 3, 4 * side + h:4 * side + h + 1],
                                 As[3][0, h, 32 * (1 - side):32 * (1 - side) + 32]
                                 .rearrange("(d one) -> d one", one=1)).then_inc(s_w_loaded, 16)
            sp.dma_start(xs[:, :, :], x.rearrange("(t p) f -> p t f", p=P)).then_inc(s_x_loaded, 16)

            def load_rows(tiles):
                for tile in tiles:
                    if due(tile.t - 2):
                        sp.wait_ge(s_adj_read, tile.t - 2)
                    sp.nop(nofuse=True)
                    sp.dma_start(adj_sb[:, tile.par * N:(tile.par + 1) * N],
                                 adj[bass.ds(tile.t * P, P), :]).then_inc(s_adj_loaded[tile.par], 16)

            sparse_tiles(sp, load_rows)
            if due(TILES - 1):
                sp.wait_ge(s_adj_read, TILES - 1)
            sp.dma_start(adj_sb[:, 0:N], adj[0:P, :]).then_inc(s_adj_tile, 16)

            def save_table(l, quad):
                sp.wait_ge(s_h_sb, quad + (l * (TILES // 4) + 1))
                sp.nop(nofuse=True)
                sp.dma_start(tables[l][bass.ds(quad * (4 * P), 4 * P), :].rearrange("(a p) c -> p a c", p=P),
                             hs[:, bass.ds(quad * 4, 4), 0:F + HEADS[l]]).then_inc(s_table, 16)

            def save_x(tile):
                sp.wait_ge(s_x_done, tile.t + 3 * TILES + 1)
                sp.nop(nofuse=True)
                sp.dma_start(out[bass.ds(tile.t * P, P), :], xs[:, tile.t, :]).then_inc(s_out, 16)

            sp.wait_ge(s_flag, 1)
            many = sp.value_load(over_int[0:1, 0:1])
            with sp.If(many < 1):
                over_quads(sp, lambda quad: save_table(0, quad))
                for l in range(LAYERS):
                    if l < 3:
                        over_plan(sp, SPARSE, lambda tiles, quad: save_table(l + 1, quad))
                    else:
                        over_plan(sp, SPARSE, lambda tiles, quad: [save_x(tile) for tile in tiles])
                sp.nop()
            with sp.Else():
                for l in range(LAYERS):
                    def dense_rows(tiles, quad):
                        tile = tiles[0]
                        n = tile.t + l * TILES
                        sp.wait_ge(s_adj_tile, (n + 1) * 16)
                        sp.nop(nofuse=True)
                        if due(tile.t * (16 * HEADS[l]) + l * (TILES * 16)):
                            sp.wait_ge(s_adj_tile_mask, tile.t * (16 * HEADS[l]) + l * (TILES * 16))
                        sp.nop(nofuse=True)
                        sp.dma_start(adj_sb[:, 0:N], adj[bass.ds(tile.t * P, P), :]).then_inc(s_adj_tile, 16)
                        if l == 3:
                            save_x(tile)
                    over_plan(sp, DENSE, dense_rows)
                sp.nop()
            sp.wait_ge(s_out, 16 * TILES)

        @block.gpsimd
        def _(pool):
            pool.memset(a_sb[:, :, :], 0.0).then_inc(s_consts, 1)
            pool.memset(ident[:, :], 0.0).then_inc(s_consts, 1)
            pool.memset(before_row[:, :], 1.0).then_inc(s_consts, 1)
            pool.memset(mean_of[:, :], 1.0 / N).then_inc(s_consts, 1)
            pool.memset(zeros[:, :], 0.0).then_inc(s_consts, 1)
            pool.memset(eps[:, :], EPS).then_inc(s_consts, 1)
            pool.memset(over[:, :, :], 0.0).then_inc(s_consts, 1)
            pool.iota(slot_numbers[:, :], pattern=[[1, SHIFT + SLOTS * P]], base=-SHIFT, channel_multiplier=0,
                      allow_small_or_imprecise_dtypes=True).then_inc(s_consts, 1)
            at = 0
            for runs in (4, 8, 16):
                bounds = run_bounds(runs)
                for i in range(runs):
                    pool.memset(base[:, at + i, :], float(bounds[i] + 1)).then_inc(s_base_fill, 1)
                at += runs
            pool.wait_ge(s_consts, 8)
            pool.affine_select(out=ident[:, :], in_=ident[:, :], compare_op=ALU.not_equal, fill=1.0,
                               base=0, pattern=[[-1, P]], channel_multiplier=1).then_inc(s_consts, 1)
            pool.affine_select(out=before_row[:, :], in_=before_row[:, :], compare_op=ALU.is_gt, fill=0.0,
                               base=0, pattern=[[1, P]], channel_multiplier=-1).then_inc(s_consts, 1)
            pool.tensor_scalar(slot_numbers[:, :], slot_numbers[:, :], UNIT, None, ALU.mult).then_inc(s_consts, 1)

            pool.wait_ge(s_flag, 1)
            many = pool.value_load(over_int[0:1, 0:1])
            with pool.If(many < 1):
                for l in range(LAYERS):
                    pool.wait_ge(s_table, 16 * (l + 1) * (TILES // 4))

                    def gather(tiles, quad):
                        for tile in tiles:
                            if tile.cls.dense:
                                continue
                            c = tile.cls
                            if tile.cls.t0 >= 4:
                                pool.wait_ge(s_agg_group, group_index(l, SPARSE, tile, 0, -3 * HEADS[l] * c.groups))
                            else:
                                if due(group_base(l, SPARSE)):
                                    pool.wait_ge(s_agg_group, group_base(l, SPARSE))
                            at = before(SPARSE, lambda k: 0 if k.dense else k.chunks, tile)
                            pool.tensor_copy(column_step[:, tile.slot, 0:c.chunks], columns[:, bass.ds(at, c.chunks)])\
                                .then_inc(s_step_copied, 1)
                            pool.wait_ge(s_step_copied, tile.t + l * (TILES - 1))
                            pool.nop(nofuse=True)
                            for i in range(c.chunks):
                                pool.indirect_dma_start(
                                    out=features(l, tile, i, 0, F + HEADS[l]), out_offset=None, in_=tables[l],
                                    in_offset=bass.IndirectOffsetOnAxis(ap=column_step[:, tile.slot, i:i + 1], axis=0))\
                                    .then_inc(s_gathered[tile.slot], 16)
                    over_plan(pool, SPARSE, gather)
                pool.nop()
            with pool.Else():
                pool.nop()

        def node_dve(dve, l, quad):
            n = quad + l * (TILES // 4)
            if l == 0:
                dve.wait_ge(s_x_loaded, 16)
            else:
                dve.wait_ge(s_x_done, (n - (TILES // 4)) * 4 + 4)
            if due(n):
                dve.wait_ge(s_z, n)
            for i in range(4):
                op = nc.vector.bn_stats(stats[:, i, :], xs[:, quad * 4 + i, :])
            op.then_inc(s_bn, 1)
            dve.wait_ge(s_bn, n + 1)
            dve.nop(nofuse=True)
            for i in range(4):
                op = nc.vector.bn_aggr(mv[:, i, :], stats[:, i, :])
            op.then_inc(s_mv, 1)
            dve.wait_ge(s_rstd, n + 1)
            if due(n):
                dve.wait_ge(s_zt, n)
            for i in range(4):
                op = nc.vector.tensor_scalar(z[:, i, :], xs[:, quad * 4 + i, :], mv[:, i, 0:1], rstd[:, i:i + 1],
                                             ALU.subtract, ALU.mult)
            op.then_inc(s_z, 1)
            w = F + 2 * HEADS[l]
            dve.wait_ge(s_hn, n + 1)
            for i, bank in enumerate((HN, ZT)):
                op = nc.vector.tensor_copy(hs[:, bass.ds(quad * 4 + 2 * i, 2), 0:w],
                                           bank[:, 0:2 * w].rearrange("p (t c) -> p t c", t=2))
            if l != 2:
                op.then_inc(s_h_sb, 1)
                return
            op.then_inc(s_h_copied, 1)
            for i, bank in enumerate((HN, ZT)):
                op = nc.vector.tensor_reduce(row_sum[:, 2 * i:2 * i + 2],
                                             bank[:, 0:2 * w].rearrange("p (t c) -> p t c", t=2)[:, :, 0:F],
                                             AX, ALU.add)
            op.then_inc(s_hsum, 1)
            dve.wait_ge(s_hsum, quad + 1)
            nc.vector.tensor_scalar(row_sum[:, :], row_sum[:, :], 0.0, -UNIT, ALU.is_equal, ALU.mult).then_inc(s_hs_low, 1)
            dve.wait_ge(s_hs_low, quad + 1)
            dve.wait_ge(s_h_copied, quad + 1)
            nc.vector.tensor_tensor(hs[:, bass.ds(quad * 4, 4), F], hs[:, bass.ds(quad * 4, 4), F], row_sum[:, :],
                                    ALU.add).then_inc(s_h_sb, 1)

        def node_act(act, l, quad):
            n = quad + l * (TILES // 4)
            act.wait_ge(s_mv, n + 1)
            if due(n):
                act.wait_ge(s_z, n)
            nc.scalar.activation(logv[:, :], mv[:, :, 1], ACT.Ln, bias=eps[:, 0:1]).then_inc(s_logv, 1)
            act.wait_ge(s_logv, n + 1)
            nc.scalar.activation(rstd[:, :], logv[:, :], ACT.Exp, scale=-0.5).then_inc(s_rstd, 1)
            act.wait_ge(s_zt, n + 1)
            if due(n):
                act.wait_ge(s_hn, n)
            nc.scalar.activation(z_t[:, :], ZT[:, :], ACT.Relu).then_inc(s_z_t, 1)

        def node_pe(pe, l, quad):
            n = quad + l * (TILES // 4)
            pe.wait_ge(s_z, n + 1)
            if due(n):
                pe.wait_ge(s_h_sb, n)
            for i in range(4):
                op = nc.tensor.transpose(ZT[:, i * P:(i + 1) * P], z[:, i, :], ident[:, :])
            op.then_inc(s_zt, 1)
            pe.wait_ge(s_z_t, n + 1)
            w = F + 2 * HEADS[l]
            for i in range(4):
                bank = (HN, ZT)[i // 2]
                op = nc.tensor.matmul(bank[:, (i % 2) * w:(i % 2 + 1) * w], z_t[:, i * P:(i + 1) * P],
                                      wext[:, l, 0:w], start=True, stop=True)
            op.then_inc(s_hn, 1)
            pe.wait_ge(s_h_sb, n + 1)
            for i in range(4):
                op = nc.tensor.matmul(MEAN[:, :], mean_of[:, :], hs[:, quad * 4 + i, 0:F], start=False, stop=False,
                                      skip_group_check=True)
            op.then_inc(s_mean_added, 1)

        def mean_begin(pe, l):
            if due(l):
                pe.wait_ge(s_hbar, l)
            nc.tensor.matmul(MEAN[:, :], zeros[:, :], zeros[:, :], start=True, stop=False, skip_group_check=True)

        def mean_end(pe, l):
            nc.tensor.matmul(MEAN[:, :], zeros[:, :], zeros[:, :], start=False, stop=True,
                             skip_group_check=True).then_inc(s_mean, 1)

        def mean_read(dve, l):
            dve.wait_ge(s_mean, l + 1)
            nc.vector.tensor_copy(hbar[:, :], MEAN[:, :]).then_inc(s_hbar, 1)

        @block.tensor
        def _(pe):
            pe.wait_ge(s_consts, 11)
            pe.wait_ge(s_w_loaded, 16 * (LAYERS + 6 + 8))
            for l in range(LAYERS):
                nc.tensor.transpose(PT[0][:, l * P:(l + 1) * P], wext[:, l, 0:F], ident[:, :]).then_inc(s_w_t, 1)
            pe.wait_ge(s_w_t_sb, 1)
            for l in range(LAYERS):
                nh = HEADS[l]
                for side in range(2):
                    at = side * (4 if l == 3 else 1)
                    op = nc.tensor.matmul(PT[1][:, l * 8 + side * nh:l * 8 + (side + 1) * nh],
                                          attn_t[:, 0, l * P:(l + 1) * P], a_sb[:, l, at:at + nh], start=True, stop=True)
            op.then_inc(s_wa, 1)
            pe.wait_ge(s_wext, 1)
            mean_begin(pe, 0)
            over_quads(pe, lambda quad: node_pe(pe, 0, quad))
            mean_end(pe, 0)

            def lists(tiles):
                for step, tile in scan_order(tiles):
                    if step == "A":
                        continue
                    if step == "B":
                        pe.wait_ge(s_deg, tile.t)
                        if due(tile.t * 2 - 2):
                            pe.wait_ge(s_first_step, tile.t * 2 - 2)
                        nc.tensor.matmul(D[0][:, 0:1], before_row[:, :], deg[:, tile.par:tile.par + 1],
                                         start=True, stop=True).then_inc(s_row_starts, 1)
                        continue
                    pe.wait_ge(s_onehot, tile.t)
                    pe.wait_ge(s_parts, tile.t)
                    if due(tile.t - 1):
                        pe.wait_ge(s_listed, tile.t - 1)
                    n = 8 * tile.cls.rounds
                    for c in range(tile.cls.chunks):
                        for k in range(n):
                            at = SHIFT - k + c * P
                            op = nc.tensor.matmul(PT[0][:, 2 * c:2 * c + 2], onehot[:, tile.par, at:at + P],
                                                  parts[:, tile.par, k, :], start=k == 0, stop=k == n - 1)
                    op.then_inc(s_lists, 1)
            sparse_tiles(pe, lists)
            pe.wait_ge(s_over, 1)
            nc.tensor.matmul(D[1][:, 0:1], mean_of[:, :], over_sum[:, :], start=True, stop=True).then_inc(s_over_all, 1)

            def work(l, plan, tiles):
                for what, (tile, h) in heads_work(l, plan, tiles):
                    (front if what == "F" else back)(l, plan, tile, h)

            def front(l, plan, tile, h):
                c = tile.cls
                if not c.dense and h == 0:
                    got = same_slot(plan, lambda k: 16 * k.chunks, tile)
                    whole = sum(16 * k.chunks for k in SPARSE[1:] for i in range(k.count)
                                if (k.t0 + i) % 4 == tile.slot)
                    pe.wait_ge(s_gathered[tile.slot], got + l * whole)
                if c.dense:
                    pe.wait_ge(s_h_sb, (l + 1) * (TILES // 4))
                for g in range(c.groups):
                    n, par = group_index(l, plan, tile, h, g), group_parity(l, plan, tile, h, g)
                    if due(bank_free(n, g, tile)):
                        pe.wait_ge(s_dscore, bank_free(n, g, tile))
                    for i in range(min(BANK, c.chunks - g * BANK)):
                        d = features(l, tile, g * BANK + i, F + h, F + h + 1)
                        op = nc.tensor.transpose(D[par][:, i * P:(i + 1) * P], d.broadcast_to([P, P]), ident[:, :])
                    op.then_inc(s_dbcast, 1)

            def back(l, plan, tile, h):
                c, u = tile.cls, unit_index(l, tile, h)
                src = attn_buffer(l, tile, h)
                if l == 2:
                    pe.wait_ge(s_normed, tile.t + 1)
                else:
                    pe.wait_ge(s_exped, u + 1)
                if h == 0:
                    done = tile.t + l * TILES
                    if due(done if c.dense or c.t0 == 1 else done - 1):
                        pe.wait_ge(s_x_done, done if c.dense or c.t0 == 1 else done - 1)
                wide = F // HEADS[l]

                def product(g):
                    n, par = group_index(l, plan, tile, h, g), group_parity(l, plan, tile, h, g)
                    pe.wait_ge(s_pt_sb, n + 1)
                    for i in range(min(BANK, c.chunks - g * BANK)):
                        j = g * BANK + i
                        op = nc.tensor.matmul(AG[tile_parity(tile)][:, h * wide:(h + 1) * wide],
                                              attn_t[:, par, i * P:(i + 1) * P],
                                              features(l, tile, j, h * wide, (h + 1) * wide),
                                              start=j == 0, stop=j == c.chunks - 1)
                    op.then_inc(s_agg_group, 1)

                for g in range(c.groups):
                    n, par = group_index(l, plan, tile, h, g), group_parity(l, plan, tile, h, g)
                    if due(bank_free(n, g, tile)):
                        pe.wait_ge(s_pt_sb, bank_free(n, g, tile))
                    for i in range(min(BANK, c.chunks - g * BANK)):
                        j = g * BANK + i
                        op = nc.tensor.transpose(PT[par][:, i * P:(i + 1) * P], src[:, j * P:(j + 1) * P], ident[:, :])
                    op.then_inc(s_pt, 1)
                    if g:
                        product(g - 1)
                product(c.groups - 1)

            pe.wait_ge(s_flag, 1)
            many = pe.value_load(over_int[0:1, 0:1])
            with pe.If(many < 1):
                for l in range(LAYERS):
                    if l < 3:
                        mean_begin(pe, l + 1)

                    def quad_work(tiles, quad):
                        work(l, SPARSE, tiles)
                        if l < 3:
                            node_pe(pe, l + 1, quad)
                    over_plan(pe, SPARSE, quad_work)
                    if l < 3:
                        mean_end(pe, l + 1)
                pe.nop()
            with pe.Else():
                for l in range(LAYERS):
                    over_plan(pe, DENSE, lambda tiles, quad: work(l, DENSE, tiles))
                    if l < 3:
                        mean_begin(pe, l + 1)
                        over_quads(pe, lambda quad: node_pe(pe, l + 1, quad))
                        mean_end(pe, l + 1)
                pe.nop()

        @block.scalar
        def _(act):
            act.preload_act_table_set("natural_log_exp_and_others")
            act.wait_ge(s_w_t, LAYERS)
            nc.scalar.activation(attn_t[:, 0, :], PT[0][:, :], ACT.Copy).then_inc(s_w_t_sb, 1)
            act.wait_ge(s_consts, 6)
            over_quads(act, lambda quad: node_act(act, 0, quad))

            def front(l, plan, tile, h):
                c, u = tile.cls, unit_index(l, tile, h)
                buf = attn_buffer(l, tile, h)[:, 0:c.chunks * P]
                p = tile_parity(tile)
                act.wait_ge(s_dscore, group_index(l, plan, tile, h, c.groups - 1) + 1)
                row = hs[:, tile.t, F + HEADS[l] + h:F + HEADS[l] + h + 1]
                nc.scalar.activation(buf, buf, ACT.Identity, bias=row).then_inc(s_scored, 1)
                act.wait_ge(s_leaky, u + 1)
                act.wait_ge(s_negmax, u + 1)
                nc.scalar.activation(buf, buf, ACT.Exp, bias=st[:, p, NEGMAX, h:h + 1],
                                     accum_out=st[:, p, SUM, h:h + 1]).then_inc(s_exped, 1)

            def back(l, plan, tile, h):
                for g in range(tile.cls.groups):
                    n, par = group_index(l, plan, tile, h, g), group_parity(l, plan, tile, h, g)
                    wide = min(BANK, tile.cls.chunks - g * BANK) * P
                    act.wait_ge(s_pt, n + 1)
                    if due(bank_free(n, g, tile)):
                        act.wait_ge(s_agg_group, bank_free(n, g, tile))
                    nc.scalar.activation(attn_t[:, par, 0:wide], PT[par][:, 0:wide], ACT.Copy).then_inc(s_pt_sb, 1)
                if l >= 2 and h == HEADS[l] - 1:
                    n = tile.t + (l - 2) * TILES
                    act.wait_ge(s_neg, n + 1)
                    nc.scalar.activation(exp_neg[:, :], neg[:, :], ACT.Exp).then_inc(s_exp_neg, 1)

            def work(l, plan, tiles):
                for what, (tile, h) in heads_work(l, plan, tiles):
                    (front if what == "F" else back)(l, plan, tile, h)

            act.wait_ge(s_flag, 1)
            many = act.value_load(over_int[0:1, 0:1])
            with act.If(many < 1):
                for l in range(LAYERS):
                    def quad_work(tiles, quad):
                        work(l, SPARSE, tiles)
                        if l < 3:
                            node_act(act, l + 1, quad)
                    over_plan(act, SPARSE, quad_work)
                act.nop()
            with act.Else():
                for l in range(LAYERS):
                    over_plan(act, DENSE, lambda tiles, quad: work(l, DENSE, tiles))
                    if l < 3:
                        over_quads(act, lambda quad: node_act(act, l + 1, quad))
                act.nop()

        @block.vector
        def _(dve):
            dve.wait_ge(s_wa, 1)
            for l in range(LAYERS):
                op = nc.vector.tensor_copy(wext[:, l, F:F + 2 * HEADS[l]], PT[1][:, l * 8:l * 8 + 2 * HEADS[l]])
            op.then_inc(s_wext, 1)
            over_quads(dve, lambda quad: node_dve(dve, 0, quad))
            mean_read(dve, 0)
            dve.wait_ge(s_consts, 11)
            dve.wait_ge(s_base_fill, 28)

            def search(tile):
                c, t = tile.cls, tile.t
                bounds = run_bounds(c.runs)
                rows = adj_sb[:, tile.par * N:(tile.par + 1) * N]
                dve.wait_ge(s_adj_loaded[tile.par], same_parity(tile) * 16)
                dve.nop(nofuse=True)
                for i in range(c.runs):
                    nc.vector.max(top[:, i, :], rows[:, bounds[i]:bounds[i + 1]]).then_inc(s_tops, 1)
                tops = before(SPARSE, lambda k: k.runs, tile)
                for i in range(c.runs):
                    dve.wait_ge(s_tops, tops + (i + 1))
                    dve.nop(nofuse=True)
                    op = nc.vector.max_index(where[:, i, :], top[:, i, :], rows[:, bounds[i]:bounds[i + 1]])
                op.then_inc(s_adj_read, 1)
                dve.wait_ge(s_adj_read, t)
                if due(t - 1):
                    dve.wait_ge(s_deg, t - 1)
                at = {4: 0, 8: 4, 16: 12}[c.runs]
                nc.vector.tensor_tensor(keys[:, 0:c.runs, :], where[:, 0:c.runs, :], base[:, at:at + c.runs, :],
                                        ALU.add).then_inc(s_keys, 1)
                nc.vector.tensor_reduce(over[:, t, 0:1], top[:, 0:c.runs, 7], AX, ALU.max)
                if due(t * 2 - 1):
                    dve.wait_ge(s_keys, t * 2 - 1)
                if due(t * 2 - 2):
                    dve.wait_ge(s_parts, t * 2 - 2)
                nc.vector.scalar_tensor_tensor(keys[:, 0:c.runs, :], top[:, 0:c.runs, :], 0.0, keys[:, 0:c.runs, :],
                                               ALU.is_gt, ALU.mult).then_inc(s_keys, 1)
                dve.wait_ge(s_keys, t * 2)
                dve.nop(nofuse=True)
                flat = keys[:, 0:c.runs, :].rearrange("p r e -> p (r e)")
                done = before(SPARSE, lambda k: max(2 * k.rounds - 1, 0), tile)
                for i in range(c.rounds):
                    nc.vector.max(picked[:, 8 * i:8 * i + 8], flat).then_inc(s_picks, 1)
                    if due(done + (2 * i + 1)):
                        dve.wait_ge(s_picks, done + (2 * i + 1))
                    dve.nop(nofuse=True)
                    if i < c.rounds - 1:
                        nc.vector.match_replace(flat, picked[:, 8 * i:8 * i + 8], flat, 0.0).then_inc(s_picks, 1)
                        if due(done + (2 * i + 2)):
                            dve.wait_ge(s_picks, done + (2 * i + 2))
                        dve.nop(nofuse=True)
                n = 8 * c.rounds
                nc.vector.tensor_copy(over[:, t, 1:2], picked[:, n - 1:n])
                if due(t - 2):
                    dve.wait_ge(s_row_starts, t - 2)
                nc.vector.tensor_scalar(keys[:, 0:MAXR, :].rearrange("p r e -> p (r e)")[:, 0:n], picked[:, 0:n], 0.0,
                                        0.0, ALU.is_gt, ALU.add, accum_out=deg[:, tile.par:tile.par + 1])\
                    .then_inc(s_deg, 1)
                if due(t - 2):
                    dve.wait_ge(s_lists, t - 2)
                nc.vector.tensor_copy(parts[:, tile.par, 0:n, 0], picked[:, 0:n]).then_inc(s_parts, 1)
                if due(t * 2 - 1):
                    dve.wait_ge(s_parts, t * 2 - 1)
                nc.vector.tensor_tensor(parts[:, tile.par, 0:n, 1], picked[:, 0:n], parts[:, tile.par, 0:n, 0],
                                        ALU.subtract).then_inc(s_parts, 1)

            def row_slots(tile):
                c, t, p = tile.cls, tile.t, tile.par
                dve.wait_ge(s_row_starts, t)
                if due(t - 1):
                    dve.wait_ge(s_onehot, t - 1)
                nc.vector.tensor_scalar(first_step[:, :], D[0][:, 0:1], UNIT, None, ALU.mult).then_inc(s_first_step, 1)
                nc.vector.tensor_scalar(first[:, bass.ds(t, 1)], D[0][:, 0:1], UNIT, None, ALU.mult)
                nc.vector.tensor_scalar(end[:, bass.ds(t, 1)], D[0][:, 0:1], deg[:, p:p + 1], UNIT, ALU.add, ALU.mult)\
                    .then_inc(s_first_step, 1)
                dve.wait_ge(s_first_step, t * 2)
                nc.vector.tensor_scalar(over[:, t, 2:3], end[:, bass.ds(t, 1)], UNIT * P * c.chunks, None, ALU.is_gt)
                wide = SHIFT + c.chunks * P
                if due(t - 2):
                    dve.wait_ge(s_lists, t - 2)
                nc.vector.tensor_scalar(onehot[:, p, 0:wide], slot_numbers[:, 0:wide], first_step[:, 0:1], None,
                                        ALU.is_equal).then_inc(s_onehot, 1)

            def write_list(tile):
                c, t = tile.cls, tile.t
                dve.wait_ge(s_lists, t)
                if due(t - 1):
                    dve.wait_ge(s_columns, t - 1)
                nc.vector.tensor_reduce(listed[:, 0:c.chunks], PT[0][:, 0:2 * c.chunks].rearrange("p (c two) -> p c two", two=2),
                                        AX, ALU.add).then_inc(s_listed, 1)
                dve.wait_ge(s_listed, t)
                at = before(SPARSE, lambda k: 0 if k.dense else k.chunks, tile)
                nc.vector.tensor_scalar(columns[:, bass.ds(at, c.chunks)], listed[:, 0:c.chunks], 1.0, -1.0,
                                        ALU.max, ALU.add).then_inc(s_columns, 1)

            def scan(tiles):
                for step, tile in scan_order(tiles):
                    {"A": search, "B": row_slots, "C": write_list}[step](tile)

            sparse_tiles(dve, scan)
            dve.wait_ge(s_columns, TILES - 1)
            dve.wait_ge(s_first_step, 2 * (TILES - 1))
            nc.vector.tensor_reduce(over_sum[:, :], over[:, :, :].rearrange("p t c -> p (t c)"), AX, ALU.max)\
                .then_inc(s_listed, 1)
            dve.wait_ge(s_listed, TILES)
            nc.vector.tensor_scalar(over_sum[:, :], over_sum[:, :], 0.0, float(N), ALU.is_gt, ALU.mult).then_inc(s_over, 1)
            dve.wait_ge(s_over_all, 1)
            nc.vector.tensor_scalar(over_int[:, :], D[1][:, 0:1], 1.0 if force_dense else 0.0, None, ALU.add)\
                .then_inc(s_flag, 1)

            def front(l, plan, tile, h):
                c, u, t = tile.cls, unit_index(l, tile, h), tile.t
                p, up = tile_parity(tile), unit_parity(l, tile, h)
                buf = attn_buffer(l, tile, h)
                wide = c.chunks * P
                if c.dense:
                    if h == 0 and plan is DENSE:
                        dve.wait_ge(s_adj_tile, (t + (l * TILES + 2)) * 16)
                    elif h == 0:
                        dve.wait_ge(s_adj_tile, 16)
                elif h == 0:
                    n = t + l * (TILES - 1)
                    m = mask[:, p, 0:wide]
                    numbers = slot_numbers[:, SHIFT:SHIFT + wide]
                    nc.vector.tensor_scalar(m, numbers, end[:, bass.ds(t, 1)], -UNIT, ALU.is_ge, ALU.mult).then_inc(s_mask_half, 1)
                    if due(n):
                        dve.wait_ge(s_mask_half, n)
                    nc.vector.scalar_tensor_tensor(m, numbers, first[:, bass.ds(t, 1)], m, ALU.subtract, ALU.min)\
                        .then_inc(s_mask, 1)
                    if due(n):
                        dve.wait_ge(s_mask, n)
                if due(groups_freed(l, plan, tile, h)):
                    dve.wait_ge(s_pt, groups_freed(l, plan, tile, h))
                for g in range(c.groups):
                    n, par = group_index(l, plan, tile, h, g), group_parity(l, plan, tile, h, g)
                    cols = min(BANK, c.chunks - g * BANK) * P
                    if c.dense:
                        m = mask[:, 0, (g % 2) * 512:(g % 2) * 512 + cols]
                        if due(n - 1):
                            dve.wait_ge(s_dscore, n - 1)
                        op = nc.vector.tensor_scalar(m, adj_sb[:, g * 512:g * 512 + cols], 0.0, -UNIT, ALU.is_le, ALU.mult)
                        op.then_inc(s_adj_tile_mask, 1)
                        dve.wait_ge(s_adj_tile_mask, dense_mask_count(l, plan, tile, h, g))
                    else:
                        m = mask[:, p, g * 512:g * 512 + cols]
                    dve.wait_ge(s_dbcast, n + 1)
                    dve.nop(nofuse=True)
                    nc.vector.tensor_tensor_reduce(out=buf[:, g * 512:g * 512 + cols], in0=D[par][:, 0:cols], in1=m,
                                                   scale=1.0, scalar=FLOOR, op0=ALU.add, op1=ALU.max,
                                                   accum_out=group_max[:, up, g:g + 1]).then_inc(s_dscore, 1)
                dve.wait_ge(s_dscore, group_index(l, plan, tile, h, c.groups - 1) + 1)
                biggest = st[:, p, BIGGEST, h:h + 1]
                nc.vector.tensor_reduce(biggest, group_max[:, up, 0:c.groups], AX, ALU.max).then_inc(s_biggest, 1)
                dve.wait_ge(s_biggest, u + 1)
                row = hs[:, t, F + HEADS[l] + h:F + HEADS[l] + h + 1]
                q = st[:, p, Q, h:h + 1]
                nc.vector.tensor_scalar(q, biggest, row, -1.0, ALU.add, ALU.mult).then_inc(s_q, 1)
                dve.wait_ge(s_q, u + 1)
                nc.vector.scalar_tensor_tensor(st[:, p, NEGMAX, h:h + 1], q, ALPHA[l], q, ALU.mult, ALU.min)\
                    .then_inc(s_negmax, 1)
                dve.wait_ge(s_scored, u + 1)
                leaky = nc.vector.scalar_tensor_tensor(buf[:, 0:wide], buf[:, 0:wide], ALPHA[l], buf[:, 0:wide],
                                                       ALU.mult, ALU.max)
                if l != 2:
                    leaky.then_inc(s_leaky, 1)
                    return
                leaky.then_inc(s_counted, 1)
                dve.wait_ge(s_counted, t + 1)
                scratch = attn_buffer(l, tile, h)[:, 2048:2048 + SLOTS * P] if not c.dense else None
                if c.dense:
                    for g in range(c.groups):
                        nc.vector.tensor_scalar(mask[:, 1, 0:512], buf[:, g * 512:(g + 1) * 512], LOW, 0.0,
                                                ALU.is_gt, ALU.add, accum_out=group_max[:, 1, g:g + 1])\
                            .then_inc(s_counted_part, 1)
                        dve.wait_ge(s_counted_part, t * c.groups + (g + 1))
                    nc.vector.tensor_reduce(st[:, p, COUNT, 0:1], group_max[:, 1, 0:c.groups], AX, ALU.add)\
                        .then_inc(s_leaky, 1)
                else:
                    nc.vector.tensor_scalar(scratch[:, 0:wide], buf[:, 0:wide], LOW, 0.0, ALU.is_gt, ALU.add,
                                            accum_out=st[:, p, COUNT, 0:1]).then_inc(s_leaky, 1)

            def back(l, plan, tile, h):
                c, u, t = tile.cls, unit_index(l, tile, h), tile.t
                p, nh = tile_parity(tile), HEADS[l]
                buf = attn_buffer(l, tile, h)[:, 0:c.chunks * P]
                if l == 2:
                    dve.wait_ge(s_exped, u + 1)
                    nc.vector.reciprocal(st[:, p, RSUM, 0:1], st[:, p, SUM, 0:1]).then_inc(s_recip, 1)
                    dve.wait_ge(s_recip, TILES * 2 + t + 1)
                    nc.vector.tensor_scalar(buf, buf, st[:, p, RSUM, 0:1], None, ALU.mult).then_inc(s_attn, 1)
                    dve.wait_ge(s_attn, t + 1)
                    nc.vector.scalar_tensor_tensor(buf, buf, THRESHOLD, buf, ALU.is_ge, ALU.mult).then_inc(s_normed, 1)
                if h < nh - 1:
                    return
                n = t + l * TILES
                if l != 2:
                    dve.wait_ge(s_exped, u + 1)
                    nc.vector.reciprocal(st[:, p, RSUM, 0:nh], st[:, p, SUM, 0:nh]).then_inc(s_recip, 1)
                nc.vector.tensor_scalar(st[:, p, VALID, 0:nh], st[:, p, BIGGEST, 0:nh], LOW, None, ALU.is_gt)
                nc.vector.tensor_scalar(st[:, p, EMPTY, 0:nh], st[:, p, BIGGEST, 0:nh], LOW, None, ALU.is_le)\
                    .then_inc(s_scale, 1)
                dve.wait_ge(s_recip, n + 1)
                dve.wait_ge(s_scale, n * 2 + 1)
                if l == 2:
                    nc.vector.scalar_tensor_tensor(st[:, p, KEEP, 0:1], st[:, p, RSUM, 0:1], THRESHOLD,
                                                   st[:, p, COUNT, 0:1], ALU.is_gt, ALU.mult).then_inc(s_fin_a, 1)
                    dve.wait_ge(s_fin_a, t + 1)
                    nc.vector.tensor_tensor(st[:, p, SCALE, 0:1], st[:, p, VALID, 0:1], st[:, p, KEEP, 0:1], ALU.mult)\
                        .then_inc(s_scale, 1)
                else:
                    nc.vector.tensor_tensor(st[:, p, SCALE, 0:nh], st[:, p, VALID, 0:nh], st[:, p, RSUM, 0:nh], ALU.mult)\
                        .then_inc(s_scale, 1)
                dve.wait_ge(s_scale, n * 2 + 2)
                dve.wait_ge(s_agg_group, group_index(l, plan, tile, h, c.groups - 1) + 1)
                ag, xt = AG[p][:, :], xs[:, t, :]
                scale, empty = st[:, p, SCALE, 0:nh], st[:, p, EMPTY, 0:nh]
                if l < 2:
                    nc.vector.scalar_tensor_tensor(y[:, :], ag, scale, xt, ALU.mult, ALU.add).then_inc(s_fin_b, 1)
                    dve.wait_ge(s_fin_b, n + 1)
                    nc.vector.scalar_tensor_tensor(xt, hbar[:, :], empty, y[:, :], ALU.mult, ALU.add)\
                        .then_inc(s_x_done, 1)
                    dve.wait_ge(s_x_done, n + 1)
                    return
                m = t + (l - 2) * TILES
                if l == 2:
                    nc.vector.scalar_tensor_tensor(y[:, :], ag, scale, hs[:, t, 0:F], ALU.mult, ALU.add)\
                        .then_inc(s_fin_y, 1)
                else:
                    by_head = ag.rearrange("p (h d) -> p h d", h=nh)
                    hb = hbar[:, :].rearrange("p (h d) -> p h d", h=nh)
                    y3, y23 = (a[:, :].rearrange("p (h d) -> p h d", h=nh) for a in (y, y2))
                    nc.vector.tensor_tensor(y3, by_head, scale.unsqueeze(2).broadcast_to([P, nh, F // nh]), ALU.mult)
                    nc.vector.tensor_tensor(y23, hb, empty.unsqueeze(2).broadcast_to([P, nh, F // nh]), ALU.mult)\
                        .then_inc(s_fin_b, 1)
                    dve.wait_ge(s_fin_b, 2 * TILES + t + 1)
                    nc.vector.tensor_tensor(y[:, :], y[:, :], y2[:, :], ALU.add).then_inc(s_fin_y, 1)
                dve.wait_ge(s_fin_y, m + 1)
                nc.vector.tensor_scalar(neg[:, :], y[:, :], 0.0, None, ALU.min).then_inc(s_neg, 1)
                dve.wait_ge(s_exp_neg, m + 1)
                nc.vector.scalar_tensor_tensor(y2[:, :], y[:, :], 0.0, exp_neg[:, :], ALU.max, ALU.add)\
                    .then_inc(s_elu, 1)
                dve.wait_ge(s_elu, m + 1)
                nc.vector.scalar_tensor_tensor(xt, y2[:, :], -1.0, xt, ALU.add, ALU.add).then_inc(s_x_done, 1)
                dve.wait_ge(s_x_done, n + 1)

            def work(l, plan, tiles):
                for what, (tile, h) in heads_work(l, plan, tiles):
                    (front if what == "F" else back)(l, plan, tile, h)

            dve.wait_ge(s_flag, 1)
            many = dve.value_load(over_int[0:1, 0:1])
            with dve.If(many < 1):
                for l in range(LAYERS):
                    def quad_work(tiles, quad):
                        work(l, SPARSE, tiles)
                        if l < 3:
                            node_dve(dve, l + 1, quad)
                    over_plan(dve, SPARSE, quad_work)
                    if l < 3:
                        mean_read(dve, l + 1)
                dve.nop()
            with dve.Else():
                for l in range(LAYERS):
                    over_plan(dve, DENSE, lambda tiles, quad: work(l, DENSE, tiles))
                    if l < 3:
                        over_quads(dve, lambda quad: node_dve(dve, l + 1, quad))
                        mean_read(dve, l + 1)
                dve.nop()


_INS = ["x", "adj", "L0_gnn_W", "L0_gnn_a", "L1_gnn_W", "L1_gnn_a", "L2_gnn_W", "L2_gnn_a", "L3_gnn_W", "L3_gnn_a"]
FORCE = False


def kernel(**inputs):
    import numpy as _np
    import concourse.bacc as _bacc
    from concourse import mybir as _mybir
    from concourse.bass_utils import run_bass_kernel_spmd as _run

    nc = _bacc.Bacc("TRN2", target_bir_lowering=False, num_devices=1)
    arrays, args = {}, []
    for name in _INS:
        a = _np.ascontiguousarray(inputs[name])
        arrays[f"in_{name}"] = a
        args.append(nc.dram_tensor(f"in_{name}", a.shape, _mybir.dt.from_np(a.dtype), kind="ExternalInput").ap())
    args.append(nc.dram_tensor("out_x", (8192, 128), _mybir.dt.float32, kind="ExternalOutput").ap())
    gat_kernel(nc, *args)
    r = _run(nc, [arrays], core_ids=[0])
    return r.results[0]["out_x"]
```

```python
from contextlib import ExitStack

import concourse.bass as bass
from concourse import mybir
from concourse.alu_op_type import AluOpType as ALU

FP32 = mybir.dt.float32
BF16 = mybir.dt.bfloat16
I32 = mybir.dt.int32
U32 = mybir.dt.uint32
ACT = mybir.ActivationFunctionType
AX = mybir.AxisListType.X

P = 128
N = 8192
F = 128
TILES = N // P
LAYERS = 4
ALPHA = [0.2, 0.01, 0.2, 0.2]
HEADS = [1, 1, 1, 4]
THRESHOLD = 1e-4
UNIT = float(2.0 ** 83)
LOW = -float(2.0 ** 60)
FLOOR = -3.0e38
EPS = 1e-5
SHIFT = 32
BANK = 4
MAXR = 4


class TileClass:

    def __init__(self, t0, count, runs, rounds, chunks):
        self.t0, self.count, self.runs, self.rounds, self.chunks = t0, count, runs, rounds, chunks
        self.groups = -(-chunks // BANK)
        self.dense = chunks == TILES


class Tile:

    def __init__(self, cls, k, off, quad=None):
        self.cls, self.k, self.off, self.quad = cls, k, off, quad
        self.t = k + cls.t0
        self.slot = (cls.t0 + off) % 4
        self.par = self.slot % 2


DENSE0 = TileClass(0, 1, 0, 0, TILES)
SPARSE = [
    DENSE0,
    TileClass(1, 1, 16, 4, 15),
    TileClass(2, 2, 16, 4, 12),
    TileClass(4, 4, 8, 3, 9),
    TileClass(8, 8, 8, 3, 7),
    TileClass(16, 16, 8, 2, 5),
    TileClass(32, 12, 4, 2, 4),
    TileClass(44, 20, 4, 2, 3),
]
DENSE = [TileClass(0, TILES, 0, 0, TILES)]
SLOTS = 15
CHUNKS = sum(c.count * c.chunks for c in SPARSE[1:])


def run_bounds(runs):
    b = [0]
    for i in range(1, runs):
        b.append(max(int(round(N * (i / runs) ** 2 / 32)) * 32, b[-1] + 32))
    return b + [N]


def before(plan, f, tile):
    total = sum(f(c) * c.count for c in plan if c.t0 < tile.cls.t0)
    return total + tile.k * f(tile.cls)


def before_parity(plan, f, tile):
    total = sum(f(c) * c.count for c in plan if c.t0 < tile.cls.t0)
    return (total + tile.off * f(tile.cls)) % 2


def same_slot(plan, f, tile):
    total = sum(f(c) for c in plan if not c.dense and c.t0 < tile.cls.t0
                for k in range(c.count) if (c.t0 + k) % 4 == tile.slot)
    if tile.cls.count < 4:
        return total + f(tile.cls)
    quad = tile.quad
    return total + quad * f(tile.cls) + f(tile.cls)


def same_parity(tile):
    if tile.cls.count < 4:
        return (tile.t + 1) // 2 if tile.par else tile.t // 2
    t = tile.cls.t0 + tile.off % 4
    return tile.quad * 2 + ((t + 1) // 2 if tile.par else t // 2)


def gat_kernel(nc, x, adj, W0, a0, W1, a1, W2, a2, W3, a3, out, force_dense=False):
    Ws, As = [W0, W1, W2, W3], [a0, a1, a2, a3]
    tables = [nc.dram_tensor(f"table{l}", [N, F + HEADS[l]], FP32).ap() for l in range(LAYERS)]
    ctx = ExitStack()
    with ctx:
        def sb(name, shape, dt):
            return ctx.enter_context(nc.sbuf_tensor(name, shape, dt))

        def pb(name, shape, dt=FP32):
            return ctx.enter_context(nc.psum_tensor(name, shape, dt))

        def sem(name):
            return ctx.enter_context(nc.semaphore(name))

        adj_sb = sb("adj_sb", [P, 2 * N], I32)
        ring = adj_sb[:, N:2 * N].bitcast(FP32)
        xs = sb("xs", [P, TILES, F], FP32)
        hs = sb("hs", [P, TILES, F + 8], FP32)
        scores = sb("scores", [P, N], FP32)
        mask = sb("mask", [P, 2, SLOTS * P], BF16)

        onehot = sb("onehot", [P, 2, SHIFT + SLOTS * P], BF16)
        valid = onehot[:, 0, :]
        slot_numbers = sb("slot_numbers", [P, SHIFT + SLOTS * P], FP32)
        columns = sb("columns", [P, CHUNKS], U32)
        column_step = sb("column_step", [P, 4, SLOTS], U32)
        attn_t = sb("attn_t", [P, 2, 512], FP32)
        z = sb("z", [P, 4, F], FP32)
        z_t = sb("z_t", [P, 4 * P], FP32)
        wext = sb("wext", [P, LAYERS, F + 8], FP32)
        a_sb = sb("a_sb", [P, LAYERS, 8], FP32)
        ident = sb("ident", [P, P], FP32)
        before_row = sb("before_row", [P, P], FP32)
        ones = sb("ones", [P, P], FP32)
        z_sum = sb("z_sum", [P, 1], FP32)
        z_total = sb("z_total", [P, 2], FP32)
        hbar = sb("hbar", [P, F], FP32)
        base = sb("base", [P, 28, 8], FP32)
        first = sb("first", [P, TILES], FP32)
        end = sb("end", [P, TILES], FP32)
        over = sb("over", [P, TILES, 3], FP32)
        top = sb("top", [P, 16, 8], FP32)
        where = sb("where", [P, 16, 8], U32)
        keys = sb("keys", [P, 16, 8], FP32)
        picked = sb("picked", [P, 8 * MAXR], FP32)
        parts = sb("parts", [P, 2, 8 * MAXR, 2], BF16)
        deg = sb("deg", [P, 2], FP32)
        first_step = sb("first_step", [P, 1], FP32)
        listed = sb("listed", [P, SLOTS], FP32)
        over_sum = sb("over_sum", [P, 1], FP32)
        over_int = sb("over_int", [P, 1], I32)
        group_max = sb("group_max", [P, 4, TILES // BANK], FP32)
        st = sb("st", [P, 4, 12, 4], FP32)
        stats = sb("stats", [P, 4, 6], FP32)
        mv = sb("mv", [P, 4, 2], FP32)
        logv = sb("logv", [P, 4], FP32)
        rstd = sb("rstd", [P, 4], FP32)
        eps = sb("eps", [P, 1], FP32)
        row_sum = sb("row_sum", [P, 4], FP32)
        y = sb("y", [P, F], FP32)
        y2 = sb("y2", [P, F], FP32)
        neg = sb("neg", [P, F], FP32)
        exp_neg = sb("exp_neg", [P, F], FP32)

        D = [pb("D0", [P, 512]), pb("D1", [P, 512])]
        PT = [pb("PT0", [P, 512]), pb("PT1", [P, 512])]
        AG = [pb("AG0", [P, F]), pb("AG1", [P, F])]
        ZT = pb("ZT", [P, 512])
        HN = pb("HN", [P, 512])

        BIGGEST, Q, NEGMAX, SUM, RSUM, VALID, SCALE, EMPTY, COUNT, KEEP = range(10)

        s_w_loaded = sem("s_w_loaded")
        s_x_loaded = sem("s_x_loaded")
        s_consts = sem("s_consts")
        s_base_fill = sem("s_base_fill")
        s_w_t = sem("s_w_t")
        s_w_t_sb = sem("s_w_t_sb")
        s_wa = sem("s_wa")
        s_wext = sem("s_wext")
        s_adj_read = sem("s_adj_read")
        s_tops = sem("s_tops")
        s_keys = sem("s_keys")
        s_picks = sem("s_picks")
        s_deg = sem("s_deg")
        s_parts = sem("s_parts")
        s_row_starts = sem("s_row_starts")
        s_first_step = sem("s_first_step")
        s_onehot = sem("s_onehot")
        s_lists = sem("s_lists")
        s_listed = sem("s_listed")
        s_columns = sem("s_columns")
        s_over = sem("s_over")
        s_over_all = sem("s_over_all")
        s_flag = sem("s_flag")
        s_adj_tile = sem("s_adj_tile")
        s_adj_tile_mask = sem("s_adj_tile_mask")
        s_step_copied = sem("s_step_copied")
        s_mask_half = sem("s_mask_half")
        s_mask = sem("s_mask")
        s_dbcast = sem("s_dbcast")
        s_dscore = sem("s_dscore")
        s_biggest = sem("s_biggest")
        s_q = sem("s_q")
        s_negmax = sem("s_negmax")
        s_scored = sem("s_scored")
        s_leaky = sem("s_leaky")
        s_counted = sem("s_counted")
        s_counted_part = sem("s_counted_part")
        s_exped = sem("s_exped")
        s_normed = sem("s_normed")
        s_attn = sem("s_attn")
        s_pt = sem("s_pt")
        s_pt_sb = sem("s_pt_sb")
        s_agg_group = sem("s_agg_group")
        s_recip = sem("s_recip")
        s_scale = sem("s_scale")
        s_fin_a = sem("s_fin_a")
        s_fin_b = sem("s_fin_b")
        s_fin_y = sem("s_fin_y")
        s_neg = sem("s_neg")
        s_exp_neg = sem("s_exp_neg")
        s_elu = sem("s_elu")
        s_x_done = sem("s_x_done")
        s_bn = sem("s_bn")
        s_mv = sem("s_mv")
        s_logv = sem("s_logv")
        s_rstd = sem("s_rstd")
        s_z = sem("s_z")
        s_zt = sem("s_zt")
        s_z_t = sem("s_z_t")
        s_hn = sem("s_hn")
        s_h_copied = sem("s_h_copied")
        s_hsum = sem("s_hsum")
        s_hs_low = sem("s_hs_low")
        s_h_sb = sem("s_h_sb")
        s_z_added = sem("s_z_added")
        s_z_mean = sem("s_z_mean")
        s_mean = sem("s_mean")
        s_hbar = sem("s_hbar")
        s_table = sem("s_table")
        s_out = sem("s_out")
        s_adj_loaded = [sem(f"s_adj_loaded{i}") for i in range(2)]
        s_gathered = [sem(f"s_gathered{i}") for i in range(4)]

        block = ctx.enter_context(nc.Block())

        def lags(l):
            return (0, 1, 2) if HEADS[l] == 1 else (1, 2, 3)

        def run_quad(l, stages, node, tiles, back_tiles, quad):
            units = [(tile, h) for tile in tiles for h in range(HEADS[l])]
            behind = [(tile, h) for tile in back_tiles for h in range(HEADS[l])][-3:]
            behind = [None] * (3 - len(behind)) + behind
            for j in range(len(units)):
                for lag, stage in stages:
                    unit = (behind + units)[3 + j - lag]
                    if unit:
                        stage(l, SPARSE, *unit)
                node(j, quad)

        def run_rest(l, stages, back_tiles):
            units = [(tile, h) for tile in back_tiles for h in range(HEADS[l])][-3:]
            for j in range(3):
                for lag, stage in stages:
                    if lag > j and 3 + j - lag < 3:
                        stage(l, SPARSE, *units[3 + j - lag])

        def run_dense(l, plan, stages, tile):
            for h in range(HEADS[l]):
                for _, stage in sorted(stages, key=lambda x: x[0]):
                    stage(l, plan, tile, h)

        def layer_units(l):
            return TILES * sum(HEADS[:l])

        def unit_index(l, tile, h):
            return tile.t * HEADS[l] + (layer_units(l) + h)

        def group_base(l, plan):
            return sum(c.count * c.groups for c in plan) * sum(HEADS[:l])

        def group_index(l, plan, tile, h, g):
            return before(plan, lambda c: c.groups, tile) * HEADS[l] + (
                group_base(l, plan) + h * tile.cls.groups + g)

        def group_parity(l, plan, tile, h, g):
            n = before_parity(plan, lambda c: c.groups, tile) * HEADS[l]
            return (n + group_base(l, plan) + h * tile.cls.groups + g) % 2

        def dense_mask_count(l, plan, tile, h, g):
            per_head = TILES // BANK
            per_layer = TILES if plan is DENSE else 1
            return tile.t * (HEADS[l] * per_head) + (per_layer * per_head * sum(HEADS[:l]) + h * per_head + g + 1)

        def bank_free(n, g, tile):
            return n if tile.cls.dense and g == 0 else n - 1

        def unit_slot(l, tile, h):
            return 0 if tile.cls.dense else h if HEADS[l] > 1 else tile.slot

        def tile_slot(tile):
            return 0 if tile.cls.dense else tile.slot

        def tile_parity(tile):
            return 0 if tile.cls.dense else tile.par

        def attn_buffer(l, tile, h):
            return scores[:, unit_slot(l, tile, h) * SLOTS * P:]

        def groups_freed(l, plan, tile, h):
            start = group_index(l, plan, tile, h, 0)
            if tile.cls.dense:
                return start
            if tile.cls.t0 < 4:
                return max(start - 3 * tile.cls.groups, group_base(l, plan) + plan[0].groups * HEADS[l])
            return start - 3 * tile.cls.groups

        def features(l, tile, c, lo, hi):
            if tile.cls.dense:
                return hs[:, c, lo:hi]
            at = tile.slot * SLOTS * (F + 4) + c * (F + HEADS[l])
            return ring[:, at + lo:at + hi]

        def over_plan(eng, plan, body):
            if plan is DENSE:
                body([Tile(plan[0], 0, 0)], None, [])
                with eng.Fori(1, TILES) as k:
                    body([Tile(plan[0], k, 0)], None, [])
                return
            tiles = [Tile(c, k, k) for c in plan[:3] for k in range(c.count)]
            body(tiles, 0, [])
            for c in plan[3:]:
                tiles, back = [Tile(c, k, k, 0) for k in range(4)], tiles
                body(tiles, c.t0 // 4, back)
                if c.count > 4:
                    with eng.Fori(1, c.count // 4) as quad:
                        body([Tile(c, quad * 4 + k, k, quad) for k in range(4)], quad + c.t0 // 4,
                             [Tile(c, quad * 4 + (k - 4), k - 4, None) for k in range(4)])
                tiles = [Tile(c, c.count - 4 + k, c.count - 4 + k, c.count // 4 - 1) for k in range(4)]
            return tiles

        def over_quads(eng, body):
            body(0)
            with eng.Fori(1, TILES // 4) as quad:
                body(quad)

        def scan_order(tiles):
            n, order = len(tiles), []
            for i in range(n + 2):
                if i < n:
                    order.append(("A", tiles[i]))
                if 0 <= i - 1 < n:
                    order.append(("B", tiles[i - 1]))
                if 0 <= i - 2 < n:
                    order.append(("C", tiles[i - 2]))
            return order

        def sparse_tiles(eng, body):
            over_plan(eng, SPARSE, lambda tiles, quad, back: body([t for t in tiles if not t.cls.dense]))

        def due(value):
            return not isinstance(value, int) or value > 0

        @block.sync
        def _(sp):
            for l in range(LAYERS):
                sp.dma_start(wext[:, l, 0:F], Ws[l]).then_inc(s_w_loaded, 16)
            sp.wait_ge(s_consts, 1)
            for l in range(3):
                sp.dma_start(a_sb[:, l, 0:1], As[l][F:2 * F, :]).then_inc(s_w_loaded, 16)
                sp.dma_start(a_sb[:, l, 1:2], As[l][0:F, :]).then_inc(s_w_loaded, 16)
            for h in range(4):
                for side in range(2):
                    sp.dma_start(a_sb[32 * h:32 * h + 32, 3, 4 * side + h:4 * side + h + 1],
                                 As[3][0, h, 32 * (1 - side):32 * (1 - side) + 32]
                                 .rearrange("(d one) -> d one", one=1)).then_inc(s_w_loaded, 16)
            sp.dma_start(xs[:, :, :], x.rearrange("(t p) f -> p t f", p=P)).then_inc(s_x_loaded, 16)

            def load_rows(tiles):
                for tile in tiles:
                    if due(tile.t - 2):
                        sp.wait_ge(s_adj_read, tile.t - 2)
                    sp.nop(nofuse=True)
                    sp.dma_start(adj_sb[:, tile.par * N:(tile.par + 1) * N],
                                 adj[bass.ds(tile.t * P, P), :]).then_inc(s_adj_loaded[tile.par], 16)

            sparse_tiles(sp, load_rows)
            if due(TILES - 1):
                sp.wait_ge(s_adj_read, TILES - 1)
            sp.dma_start(adj_sb[:, 0:N], adj[0:P, :]).then_inc(s_adj_tile, 16)

            def save_table(l, quad):
                sp.wait_ge(s_h_sb, quad + (l * (TILES // 4) + 1))
                sp.nop(nofuse=True)
                sp.dma_start(tables[l][bass.ds(quad * (4 * P), 4 * P), :].rearrange("(a p) c -> p a c", p=P),
                             hs[:, bass.ds(quad * 4, 4), 0:F + HEADS[l]]).then_inc(s_table, 16)

            def save_x(tile):
                sp.wait_ge(s_x_done, tile.t + 3 * TILES + 1)
                sp.nop(nofuse=True)
                sp.dma_start(out[bass.ds(tile.t * P, P), :], xs[:, tile.t, :]).then_inc(s_out, 16)

            sp.wait_ge(s_flag, 1)
            many = sp.value_load(over_int[0:1, 0:1])
            with sp.If(many < 1):
                over_quads(sp, lambda quad: save_table(0, quad))
                for l in range(LAYERS):
                    if l < 3:
                        over_plan(sp, SPARSE, lambda tiles, quad, back: save_table(l + 1, quad))
                    else:
                        over_plan(sp, SPARSE, lambda tiles, quad, back: [save_x(tile) for tile in tiles])
                sp.nop()
            with sp.Else():
                for l in range(LAYERS):
                    def dense_rows(tiles, quad, back):
                        tile = tiles[0]
                        n = tile.t + l * TILES
                        sp.wait_ge(s_adj_tile, (n + 1) * 16)
                        sp.nop(nofuse=True)
                        if due(tile.t * (16 * HEADS[l]) + l * (TILES * 16)):
                            sp.wait_ge(s_adj_tile_mask, tile.t * (16 * HEADS[l]) + l * (TILES * 16))
                        sp.nop(nofuse=True)
                        sp.dma_start(adj_sb[:, 0:N], adj[bass.ds(tile.t * P, P), :]).then_inc(s_adj_tile, 16)
                        if l == 3:
                            save_x(tile)
                    over_plan(sp, DENSE, dense_rows)
                sp.nop()
            sp.wait_ge(s_out, 16 * TILES)

        @block.gpsimd
        def _(pool):
            pool.memset(a_sb[:, :, :], 0.0).then_inc(s_consts, 1)
            pool.memset(ident[:, :], 0.0).then_inc(s_consts, 1)
            pool.memset(before_row[:, :], 1.0).then_inc(s_consts, 1)
            pool.memset(ones[:, :], 1.0).then_inc(s_consts, 1)
            pool.memset(z_total[:, :], 0.0).then_inc(s_consts, 1)
            pool.memset(eps[:, :], EPS).then_inc(s_consts, 1)
            pool.memset(over[:, :, :], 0.0).then_inc(s_consts, 1)
            pool.iota(slot_numbers[:, :], pattern=[[1, SHIFT + SLOTS * P]], base=-SHIFT, channel_multiplier=0,
                      allow_small_or_imprecise_dtypes=True).then_inc(s_consts, 1)
            at = 0
            for runs in (4, 8, 16):
                bounds = run_bounds(runs)
                for i in range(runs):
                    pool.memset(base[:, at + i, :], float(bounds[i] + 1)).then_inc(s_base_fill, 1)
                at += runs
            pool.wait_ge(s_consts, 8)
            pool.affine_select(out=ident[:, :], in_=ident[:, :], compare_op=ALU.not_equal, fill=1.0,
                               base=0, pattern=[[-1, P]], channel_multiplier=1).then_inc(s_consts, 1)
            pool.affine_select(out=before_row[:, :], in_=before_row[:, :], compare_op=ALU.is_gt, fill=0.0,
                               base=0, pattern=[[1, P]], channel_multiplier=-1).then_inc(s_consts, 1)
            pool.tensor_scalar(slot_numbers[:, :], slot_numbers[:, :], UNIT, None, ALU.mult).then_inc(s_consts, 1)

            pool.wait_ge(s_flag, 1)
            many = pool.value_load(over_int[0:1, 0:1])
            with pool.If(many < 1):
                for l in range(LAYERS):
                    pool.wait_ge(s_table, 16 * (l + 1) * (TILES // 4))

                    def gather(tiles, quad, back):
                        for tile in tiles:
                            if tile.cls.dense:
                                continue
                            c = tile.cls
                            if tile.cls.t0 >= 4:
                                pool.wait_ge(s_agg_group, group_index(l, SPARSE, tile, 0, -3 * HEADS[l] * c.groups))
                            else:
                                if due(group_base(l, SPARSE)):
                                    pool.wait_ge(s_agg_group, group_base(l, SPARSE))
                            at = before(SPARSE, lambda k: 0 if k.dense else k.chunks, tile)
                            pool.tensor_copy(column_step[:, tile.slot, 0:c.chunks], columns[:, bass.ds(at, c.chunks)])\
                                .then_inc(s_step_copied, 1)
                            pool.wait_ge(s_step_copied, tile.t + l * (TILES - 1))
                            pool.nop(nofuse=True)
                            for i in range(c.chunks):
                                pool.indirect_dma_start(
                                    out=features(l, tile, i, 0, F + HEADS[l]), out_offset=None, in_=tables[l],
                                    in_offset=bass.IndirectOffsetOnAxis(ap=column_step[:, tile.slot, i:i + 1], axis=0))\
                                    .then_inc(s_gathered[tile.slot], 16)
                    over_plan(pool, SPARSE, gather)
                pool.nop()
            with pool.Else():
                pool.nop()

        def node_stats(dve, l, quad):
            n = quad + l * (TILES // 4)
            if l == 0:
                dve.wait_ge(s_x_loaded, 16)
            else:
                dve.wait_ge(s_x_done, (n - (TILES // 4)) * 4 + 4)
            if due(n):
                dve.wait_ge(s_z, n)
            for i in range(4):
                op = nc.vector.bn_stats(stats[:, i, :], xs[:, quad * 4 + i, :])
            op.then_inc(s_bn, 1)
            dve.wait_ge(s_bn, n + 1)
            dve.nop(nofuse=True)
            for i in range(4):
                op = nc.vector.bn_aggr(mv[:, i, :], stats[:, i, :])
            op.then_inc(s_mv, 1)

        def node_rstd(act, l, quad):
            n = quad + l * (TILES // 4)
            act.wait_ge(s_mv, n + 1)
            if due(n):
                act.wait_ge(s_z, n)
            nc.scalar.activation(logv[:, :], mv[:, :, 1], ACT.Ln, bias=eps[:, 0:1]).then_inc(s_logv, 1)
            act.wait_ge(s_logv, n + 1)
            nc.scalar.activation(rstd[:, :], logv[:, :], ACT.Exp, scale=-0.5).then_inc(s_rstd, 1)

        def node_normal(dve, l, quad):
            n = quad + l * (TILES // 4)
            dve.wait_ge(s_rstd, n + 1)
            if due(n):
                dve.wait_ge(s_zt, n)
            for i in range(4):
                op = nc.vector.tensor_scalar(z[:, i, :], xs[:, quad * 4 + i, :], mv[:, i, 0:1], rstd[:, i:i + 1],
                                             ALU.subtract, ALU.mult)
            op.then_inc(s_z, 1)

        def node_transpose(pe, l, quad):
            n = quad + l * (TILES // 4)
            pe.wait_ge(s_z, n + 1)
            if due(n):
                pe.wait_ge(s_h_sb, n)
            for i in range(4):
                op = nc.tensor.transpose(ZT[:, i * P:(i + 1) * P], z[:, i, :], ident[:, :])
            op.then_inc(s_zt, 1)

        def node_relu(act, l, quad):
            n = quad + l * (TILES // 4)
            act.wait_ge(s_zt, n + 1)
            if due(n):
                act.wait_ge(s_hn, n)
                act.wait_ge(s_z_added, n)
            nc.scalar.activation(z_t[:, :], ZT[:, :], ACT.Relu, accum_out=z_sum[:, 0:1]).then_inc(s_z_t, 1)

        def node_product(pe, l, quad):
            n = quad + l * (TILES // 4)
            pe.wait_ge(s_z_t, n + 1)
            if due(l):
                pe.wait_ge(s_hbar, l)
            w = F + 2 * HEADS[l]
            for i in range(4):
                bank = (HN, ZT)[i // 2]
                op = nc.tensor.matmul(bank[:, (i % 2) * w:(i % 2 + 1) * w], z_t[:, i * P:(i + 1) * P],
                                      wext[:, l, 0:w], start=True, stop=True)
            op.then_inc(s_hn, 1)

        def node_keep(dve, l, quad):
            n = quad + l * (TILES // 4)
            w = F + 2 * HEADS[l]
            dve.wait_ge(s_z_t, n + 1)
            if due(n):
                dve.wait_ge(s_z_added, n)
            nc.vector.tensor_tensor(z_total[:, 0:1], z_total[:, 0:1], z_sum[:, 0:1], ALU.add).then_inc(s_z_added, 1)
            dve.wait_ge(s_hn, n + 1)
            for i, bank in enumerate((HN, ZT)):
                op = nc.vector.tensor_copy(hs[:, bass.ds(quad * 4 + 2 * i, 2), 0:w],
                                           bank[:, 0:2 * w].rearrange("p (t c) -> p t c", t=2))
            if l != 2:
                op.then_inc(s_h_sb, 1)
                return
            op.then_inc(s_h_copied, 1)
            for i, bank in enumerate((HN, ZT)):
                op = nc.vector.tensor_reduce(row_sum[:, 2 * i:2 * i + 2],
                                             bank[:, 0:2 * w].rearrange("p (t c) -> p t c", t=2)[:, :, 0:F],
                                             AX, ALU.add)
            op.then_inc(s_hsum, 1)
            dve.wait_ge(s_hsum, quad + 1)
            nc.vector.tensor_scalar(row_sum[:, :], row_sum[:, :], 0.0, -UNIT, ALU.is_equal, ALU.mult).then_inc(s_hs_low, 1)
            dve.wait_ge(s_hs_low, quad + 1)
            dve.wait_ge(s_h_copied, quad + 1)
            nc.vector.tensor_tensor(hs[:, bass.ds(quad * 4, 4), F], hs[:, bass.ds(quad * 4, 4), F], row_sum[:, :],
                                    ALU.add).then_inc(s_h_sb, 1)

        def node_parts(eng, l, parts):
            def node(step, quad):
                for at, back, part in parts:
                    if at == step and not (isinstance(quad, int) and quad < back):
                        part(eng, l, quad - back)
            return node if l < LAYERS else lambda step, quad: None

        def mean_begin(dve, l):
            dve.wait_ge(s_z_added, (l + 1) * (TILES // 4))
            nc.vector.tensor_scalar(z_total[:, 1:2], z_total[:, 0:1], 1.0 / N, None, ALU.mult).then_inc(s_z_mean, 1)
            dve.wait_ge(s_z_mean, l + 1)
            nc.vector.memset(z_total[:, 0:1], 0.0)

        def mean_product(pe, l):
            pe.wait_ge(s_z_mean, l + 1)
            pe.wait_ge(s_h_sb, (l + 1) * (TILES // 4))
            nc.tensor.matmul(HN[:, 0:F], z_total[:, 1:2].broadcast_to([P, P]), wext[:, l, 0:F],
                             start=True, stop=True).then_inc(s_mean, 1)

        def mean_keep(dve, l):
            dve.wait_ge(s_mean, l + 1)
            nc.vector.tensor_copy(hbar[:, :], HN[:, 0:F]).then_inc(s_hbar, 1)

        @block.tensor
        def _(pe):
            pe.wait_ge(s_consts, 11)
            pe.wait_ge(s_w_loaded, 16 * (LAYERS + 6 + 8))
            for l in range(LAYERS):
                nc.tensor.transpose(PT[0][:, l * P:(l + 1) * P], wext[:, l, 0:F], ident[:, :]).then_inc(s_w_t, 1)
            pe.wait_ge(s_w_t_sb, 1)
            for l in range(LAYERS):
                nh = HEADS[l]
                for side in range(2):
                    at = side * (4 if l == 3 else 1)
                    op = nc.tensor.matmul(PT[1][:, l * 8 + side * nh:l * 8 + (side + 1) * nh],
                                          attn_t[:, 0, l * P:(l + 1) * P], a_sb[:, l, at:at + nh], start=True, stop=True)
            op.then_inc(s_wa, 1)
            pe.wait_ge(s_wext, 1)
            def node_all(quad):
                node_transpose(pe, 0, quad)
                node_product(pe, 0, quad)
            over_quads(pe, node_all)
            mean_product(pe, 0)

            def lists(tiles):
                for step, tile in scan_order(tiles):
                    if step == "A":
                        continue
                    if step == "B":
                        pe.wait_ge(s_deg, tile.t)
                        if due(tile.t * 2 - 2):
                            pe.wait_ge(s_first_step, tile.t * 2 - 2)
                        nc.tensor.matmul(D[0][:, 0:1], before_row[:, :], deg[:, tile.par:tile.par + 1],
                                         start=True, stop=True).then_inc(s_row_starts, 1)
                        continue
                    pe.wait_ge(s_onehot, tile.t)
                    pe.wait_ge(s_parts, tile.t)
                    if due(tile.t - 1):
                        pe.wait_ge(s_listed, tile.t - 1)
                    n = 8 * tile.cls.rounds
                    for c in range(tile.cls.chunks):
                        for k in range(n):
                            at = SHIFT - k + c * P
                            op = nc.tensor.matmul(PT[0][:, 2 * c:2 * c + 2], onehot[:, tile.par, at:at + P],
                                                  parts[:, tile.par, k, :], start=k == 0, stop=k == n - 1)
                    op.then_inc(s_lists, 1)
            sparse_tiles(pe, lists)
            pe.wait_ge(s_over, 1)
            nc.tensor.matmul(D[1][:, 0:1], ones[:, :], over_sum[:, :], start=True, stop=True).then_inc(s_over_all, 1)

            def front(l, plan, tile, h):
                c = tile.cls
                if not c.dense and h == 0:
                    got = same_slot(plan, lambda k: 16 * k.chunks, tile)
                    whole = sum(16 * k.chunks for k in SPARSE[1:] for i in range(k.count)
                                if (k.t0 + i) % 4 == tile.slot)
                    pe.wait_ge(s_gathered[tile.slot], got + l * whole)
                if c.dense:
                    pe.wait_ge(s_h_sb, (l + 1) * (TILES // 4))
                for g in range(c.groups):
                    n, par = group_index(l, plan, tile, h, g), group_parity(l, plan, tile, h, g)
                    if due(bank_free(n, g, tile)):
                        pe.wait_ge(s_dscore, bank_free(n, g, tile))
                    for i in range(min(BANK, c.chunks - g * BANK)):
                        d = features(l, tile, g * BANK + i, F + h, F + h + 1)
                        op = nc.tensor.transpose(D[par][:, i * P:(i + 1) * P], d.broadcast_to([P, P]), ident[:, :])
                    op.then_inc(s_dbcast, 1)

            def products(l, plan, tile, h):
                c, u = tile.cls, unit_index(l, tile, h)
                src = attn_buffer(l, tile, h)
                if l == 2:
                    pe.wait_ge(s_normed, tile.t + 1)
                else:
                    pe.wait_ge(s_exped, u + 1)
                if h == 0:
                    done = tile.t + l * TILES
                    if due(done if c.dense else done - 1):
                        pe.wait_ge(s_x_done, done if c.dense else done - 1)
                wide = F // HEADS[l]

                def product(g):
                    n, par = group_index(l, plan, tile, h, g), group_parity(l, plan, tile, h, g)
                    pe.wait_ge(s_pt_sb, n + 1)
                    for i in range(min(BANK, c.chunks - g * BANK)):
                        j = g * BANK + i
                        op = nc.tensor.matmul(AG[tile_parity(tile)][:, h * wide:(h + 1) * wide],
                                              attn_t[:, par, i * P:(i + 1) * P],
                                              features(l, tile, j, h * wide, (h + 1) * wide),
                                              start=j == 0, stop=j == c.chunks - 1)
                    op.then_inc(s_agg_group, 1)

                for g in range(c.groups):
                    n, par = group_index(l, plan, tile, h, g), group_parity(l, plan, tile, h, g)
                    if due(bank_free(n, g, tile)):
                        pe.wait_ge(s_pt_sb, bank_free(n, g, tile))
                    for i in range(min(BANK, c.chunks - g * BANK)):
                        j = g * BANK + i
                        op = nc.tensor.transpose(PT[par][:, i * P:(i + 1) * P], src[:, j * P:(j + 1) * P], ident[:, :])
                    op.then_inc(s_pt, 1)
                    if g:
                        product(g - 1)
                product(c.groups - 1)

            pe.wait_ge(s_flag, 1)
            many = pe.value_load(over_int[0:1, 0:1])
            with pe.If(many < 1):
                for l in range(LAYERS):
                    stages = [(0, front), (lags(l)[1], products)]
                    node_work = [(0, 2, node_product), (3, 1, node_transpose)]

                    def quad_work(tiles, quad, back_tiles):
                        if tiles[0].cls.dense:
                            run_dense(l, SPARSE, stages, tiles.pop(0))
                        run_quad(l, stages, node_parts(pe, l + 1, node_work), tiles, back_tiles, quad)
                    last = over_plan(pe, SPARSE, quad_work)
                    run_rest(l, stages, last)
                    if l < 3:
                        node_product(pe, l + 1, TILES // 4 - 2)
                        node_transpose(pe, l + 1, TILES // 4 - 1)
                        node_product(pe, l + 1, TILES // 4 - 1)
                        mean_product(pe, l + 1)
                pe.nop()
            with pe.Else():
                for l in range(LAYERS):
                    stages = [(0, front), (1, products)]
                    over_plan(pe, DENSE, lambda tiles, quad, back: run_dense(l, DENSE, stages, tiles[0]))
                    if l < 3:
                        def node_both(quad):
                            node_transpose(pe, l + 1, quad)
                            node_product(pe, l + 1, quad)
                        over_quads(pe, node_both)
                        mean_product(pe, l + 1)
                pe.nop()

        @block.scalar
        def _(act):
            act.preload_act_table_set("natural_log_exp_and_others")
            act.wait_ge(s_w_t, LAYERS)
            nc.scalar.activation(attn_t[:, 0, :], PT[0][:, :], ACT.Copy).then_inc(s_w_t_sb, 1)
            act.wait_ge(s_consts, 6)

            def node_first(quad):
                node_rstd(act, 0, quad)
                node_relu(act, 0, quad)
            over_quads(act, node_first)

            def shift(l, plan, tile, h):
                c = tile.cls
                buf = attn_buffer(l, tile, h)[:, 0:c.chunks * P]
                act.wait_ge(s_dscore, group_index(l, plan, tile, h, c.groups - 1) + 1)
                row = hs[:, tile.t, F + HEADS[l] + h:F + HEADS[l] + h + 1]
                nc.scalar.activation(buf, buf, ACT.Identity, bias=row).then_inc(s_scored, 1)

            def exponent(l, plan, tile, h):
                u, p = unit_index(l, tile, h), tile_slot(tile)
                buf = attn_buffer(l, tile, h)[:, 0:tile.cls.chunks * P]
                act.wait_ge(s_leaky, u + 1)
                act.wait_ge(s_negmax, u + 1)
                nc.scalar.activation(buf, buf, ACT.Exp, bias=st[:, p, NEGMAX, h:h + 1],
                                     accum_out=st[:, p, SUM, h:h + 1]).then_inc(s_exped, 1)

            def evacuate(l, plan, tile, h):
                for g in range(tile.cls.groups):
                    n, par = group_index(l, plan, tile, h, g), group_parity(l, plan, tile, h, g)
                    wide = min(BANK, tile.cls.chunks - g * BANK) * P
                    act.wait_ge(s_pt, n + 1)
                    if due(bank_free(n, g, tile)):
                        act.wait_ge(s_agg_group, bank_free(n, g, tile))
                    nc.scalar.activation(attn_t[:, par, 0:wide], PT[par][:, 0:wide], ACT.Copy).then_inc(s_pt_sb, 1)

            def negative_exp(l, plan, tile, h):
                if l < 2 or h < HEADS[l] - 1:
                    return
                act.wait_ge(s_neg, tile.t + ((l - 2) * TILES + 1))
                nc.scalar.activation(exp_neg[:, :], neg[:, :], ACT.Exp).then_inc(s_exp_neg, 1)

            act.wait_ge(s_flag, 1)
            many = act.value_load(over_int[0:1, 0:1])
            with act.If(many < 1):
                for l in range(LAYERS):
                    soon, later, last_lag = lags(l)
                    stages = [(0, shift), (last_lag, negative_exp), (later, evacuate), (soon, exponent)]
                    node_work = [(2, 1, node_rstd), (3, 1, node_relu)]

                    def quad_work(tiles, quad, back_tiles):
                        if tiles[0].cls.dense:
                            run_dense(l, SPARSE, [(0, shift), (1, exponent), (2, evacuate), (3, negative_exp)], tiles.pop(0))
                        run_quad(l, stages, node_parts(act, l + 1, node_work), tiles, back_tiles, quad)
                    last = over_plan(act, SPARSE, quad_work)
                    run_rest(l, stages, last)
                    if l < 3:
                        node_rstd(act, l + 1, TILES // 4 - 1)
                        node_relu(act, l + 1, TILES // 4 - 1)
                act.nop()
            with act.Else():
                for l in range(LAYERS):
                    stages = [(0, shift), (1, exponent), (2, evacuate), (3, negative_exp)]
                    over_plan(act, DENSE, lambda tiles, quad, back: run_dense(l, DENSE, stages, tiles[0]))
                    if l < 3:
                        def node_both(quad):
                            node_rstd(act, l + 1, quad)
                            node_relu(act, l + 1, quad)
                        over_quads(act, node_both)
                act.nop()

        @block.vector
        def _(dve):
            dve.wait_ge(s_wa, 1)
            for l in range(LAYERS):
                op = nc.vector.tensor_copy(wext[:, l, F:F + 2 * HEADS[l]], PT[1][:, l * 8:l * 8 + 2 * HEADS[l]])
            op.then_inc(s_wext, 1)
            dve.wait_ge(s_consts, 11)

            def node_first(quad):
                node_stats(dve, 0, quad)
                node_normal(dve, 0, quad)
                node_keep(dve, 0, quad)
            over_quads(dve, node_first)
            mean_begin(dve, 0)
            mean_keep(dve, 0)
            dve.wait_ge(s_base_fill, 28)

            def search(tile):
                c, t = tile.cls, tile.t
                bounds = run_bounds(c.runs)
                rows = adj_sb[:, tile.par * N:(tile.par + 1) * N]
                dve.wait_ge(s_adj_loaded[tile.par], same_parity(tile) * 16)
                dve.nop(nofuse=True)
                for i in range(c.runs):
                    nc.vector.max(top[:, i, :], rows[:, bounds[i]:bounds[i + 1]]).then_inc(s_tops, 1)
                tops = before(SPARSE, lambda k: k.runs, tile)
                for i in range(c.runs):
                    dve.wait_ge(s_tops, tops + (i + 1))
                    dve.nop(nofuse=True)
                    op = nc.vector.max_index(where[:, i, :], top[:, i, :], rows[:, bounds[i]:bounds[i + 1]])
                op.then_inc(s_adj_read, 1)
                dve.wait_ge(s_adj_read, t)
                if due(t - 1):
                    dve.wait_ge(s_deg, t - 1)
                at = {4: 0, 8: 4, 16: 12}[c.runs]
                nc.vector.tensor_tensor(keys[:, 0:c.runs, :], where[:, 0:c.runs, :], base[:, at:at + c.runs, :],
                                        ALU.add).then_inc(s_keys, 1)
                nc.vector.tensor_reduce(over[:, t, 0:1], top[:, 0:c.runs, 7], AX, ALU.max)
                if due(t * 2 - 1):
                    dve.wait_ge(s_keys, t * 2 - 1)
                if due(t * 2 - 2):
                    dve.wait_ge(s_parts, t * 2 - 2)
                nc.vector.scalar_tensor_tensor(keys[:, 0:c.runs, :], top[:, 0:c.runs, :], 0.0, keys[:, 0:c.runs, :],
                                               ALU.is_gt, ALU.mult).then_inc(s_keys, 1)
                dve.wait_ge(s_keys, t * 2)
                dve.nop(nofuse=True)
                flat = keys[:, 0:c.runs, :].rearrange("p r e -> p (r e)")
                done = before(SPARSE, lambda k: max(2 * k.rounds - 1, 0), tile)
                for i in range(c.rounds):
                    nc.vector.max(picked[:, 8 * i:8 * i + 8], flat).then_inc(s_picks, 1)
                    if due(done + (2 * i + 1)):
                        dve.wait_ge(s_picks, done + (2 * i + 1))
                    dve.nop(nofuse=True)
                    if i < c.rounds - 1:
                        nc.vector.match_replace(flat, picked[:, 8 * i:8 * i + 8], flat, 0.0).then_inc(s_picks, 1)
                        if due(done + (2 * i + 2)):
                            dve.wait_ge(s_picks, done + (2 * i + 2))
                        dve.nop(nofuse=True)
                n = 8 * c.rounds
                nc.vector.tensor_copy(over[:, t, 1:2], picked[:, n - 1:n])
                if due(t - 2):
                    dve.wait_ge(s_row_starts, t - 2)
                nc.vector.tensor_scalar(keys[:, 0:MAXR, :].rearrange("p r e -> p (r e)")[:, 0:n], picked[:, 0:n], 0.0,
                                        0.0, ALU.is_gt, ALU.add, accum_out=deg[:, tile.par:tile.par + 1])\
                    .then_inc(s_deg, 1)
                if due(t - 2):
                    dve.wait_ge(s_lists, t - 2)
                nc.vector.tensor_copy(parts[:, tile.par, 0:n, 0], picked[:, 0:n]).then_inc(s_parts, 1)
                if due(t * 2 - 1):
                    dve.wait_ge(s_parts, t * 2 - 1)
                nc.vector.tensor_tensor(parts[:, tile.par, 0:n, 1], picked[:, 0:n], parts[:, tile.par, 0:n, 0],
                                        ALU.subtract).then_inc(s_parts, 1)

            def row_slots(tile):
                c, t, p = tile.cls, tile.t, tile.par
                dve.wait_ge(s_row_starts, t)
                if due(t - 1):
                    dve.wait_ge(s_onehot, t - 1)
                nc.vector.tensor_scalar(first_step[:, :], D[0][:, 0:1], UNIT, None, ALU.mult).then_inc(s_first_step, 1)
                nc.vector.tensor_scalar(first[:, bass.ds(t, 1)], D[0][:, 0:1], UNIT, None, ALU.mult)
                nc.vector.tensor_scalar(end[:, bass.ds(t, 1)], D[0][:, 0:1], deg[:, p:p + 1], UNIT, ALU.add, ALU.mult)\
                    .then_inc(s_first_step, 1)
                dve.wait_ge(s_first_step, t * 2)
                nc.vector.tensor_scalar(over[:, t, 2:3], end[:, bass.ds(t, 1)], UNIT * P * c.chunks, None, ALU.is_gt)
                wide = SHIFT + c.chunks * P
                if due(t - 2):
                    dve.wait_ge(s_lists, t - 2)
                nc.vector.tensor_scalar(onehot[:, p, 0:wide], slot_numbers[:, 0:wide], first_step[:, 0:1], None,
                                        ALU.is_equal).then_inc(s_onehot, 1)

            def write_list(tile):
                c, t = tile.cls, tile.t
                dve.wait_ge(s_lists, t)
                if due(t - 1):
                    dve.wait_ge(s_columns, t - 1)
                nc.vector.tensor_reduce(listed[:, 0:c.chunks], PT[0][:, 0:2 * c.chunks].rearrange("p (c two) -> p c two", two=2),
                                        AX, ALU.add).then_inc(s_listed, 1)
                dve.wait_ge(s_listed, t)
                at = before(SPARSE, lambda k: 0 if k.dense else k.chunks, tile)
                nc.vector.tensor_scalar(columns[:, bass.ds(at, c.chunks)], listed[:, 0:c.chunks], 1.0, -1.0,
                                        ALU.max, ALU.add).then_inc(s_columns, 1)

            def scan(tiles):
                for step, tile in scan_order(tiles):
                    {"A": search, "B": row_slots, "C": write_list}[step](tile)

            sparse_tiles(dve, scan)
            dve.wait_ge(s_columns, TILES - 1)
            dve.wait_ge(s_first_step, 2 * (TILES - 1))
            nc.vector.tensor_reduce(over_sum[:, :], over[:, :, :].rearrange("p t c -> p (t c)"), AX, ALU.max)\
                .then_inc(s_listed, 1)
            dve.wait_ge(s_listed, TILES)
            nc.vector.tensor_scalar(over_sum[:, :], over_sum[:, :], 0.0, 1.0, ALU.is_gt, ALU.mult).then_inc(s_over, 1)
            dve.wait_ge(s_over_all, 1)
            nc.vector.tensor_scalar(over_int[:, :], D[1][:, 0:1], 1.0 if force_dense else 0.0, None, ALU.add)\
                .then_inc(s_flag, 1)

            def front(l, plan, tile, h):
                c, u, t = tile.cls, unit_index(l, tile, h), tile.t
                p, up = tile_slot(tile), unit_slot(l, tile, h)
                buf = attn_buffer(l, tile, h)
                wide = c.chunks * P
                if c.dense:
                    if h == 0 and plan is DENSE:
                        dve.wait_ge(s_adj_tile, (t + (l * TILES + 2)) * 16)
                    elif h == 0:
                        dve.wait_ge(s_adj_tile, 16)
                elif h == 0:
                    n = t + l * (TILES - 1)
                    m = mask[:, tile.par, 0:wide]
                    numbers = slot_numbers[:, SHIFT:SHIFT + wide]
                    nc.vector.tensor_scalar(m, numbers, end[:, bass.ds(t, 1)], -UNIT, ALU.is_ge, ALU.mult).then_inc(s_mask_half, 1)
                    if due(n):
                        dve.wait_ge(s_mask_half, n)
                    nc.vector.scalar_tensor_tensor(m, numbers, first[:, bass.ds(t, 1)], m, ALU.subtract, ALU.min)\
                        .then_inc(s_mask, 1)
                    if due(n):
                        dve.wait_ge(s_mask, n)
                if due(groups_freed(l, plan, tile, h)):
                    dve.wait_ge(s_pt, groups_freed(l, plan, tile, h))
                for g in range(c.groups):
                    n, par = group_index(l, plan, tile, h, g), group_parity(l, plan, tile, h, g)
                    cols = min(BANK, c.chunks - g * BANK) * P
                    if c.dense:
                        m = mask[:, 0, (g % 2) * 512:(g % 2) * 512 + cols]
                        if due(n - 1):
                            dve.wait_ge(s_dscore, n - 1)
                        op = nc.vector.tensor_scalar(m, adj_sb[:, g * 512:g * 512 + cols], 0.0, -UNIT, ALU.is_le, ALU.mult)
                        op.then_inc(s_adj_tile_mask, 1)
                        dve.wait_ge(s_adj_tile_mask, dense_mask_count(l, plan, tile, h, g))
                    else:
                        m = mask[:, tile.par, g * 512:g * 512 + cols]
                    dve.wait_ge(s_dbcast, n + 1)
                    dve.nop(nofuse=True)
                    nc.vector.tensor_tensor_reduce(out=buf[:, g * 512:g * 512 + cols], in0=D[par][:, 0:cols], in1=m,
                                                   scale=1.0, scalar=FLOOR, op0=ALU.add, op1=ALU.max,
                                                   accum_out=group_max[:, up, g:g + 1]).then_inc(s_dscore, 1)
                dve.wait_ge(s_dscore, group_index(l, plan, tile, h, c.groups - 1) + 1)
                biggest = st[:, p, BIGGEST, h:h + 1]
                nc.vector.tensor_reduce(biggest, group_max[:, up, 0:c.groups], AX, ALU.max).then_inc(s_biggest, 1)
                dve.wait_ge(s_biggest, u + 1)
                row = hs[:, t, F + HEADS[l] + h:F + HEADS[l] + h + 1]
                q = st[:, p, Q, h:h + 1]
                nc.vector.tensor_scalar(q, biggest, row, -1.0, ALU.add, ALU.mult).then_inc(s_q, 1)
                dve.wait_ge(s_q, u + 1)
                nc.vector.scalar_tensor_tensor(st[:, p, NEGMAX, h:h + 1], q, ALPHA[l], q, ALU.mult, ALU.min)\
                    .then_inc(s_negmax, 1)

            def leaky_relu(l, plan, tile, h):
                c, u, t, p = tile.cls, unit_index(l, tile, h), tile.t, tile_slot(tile)
                wide = c.chunks * P
                buf = attn_buffer(l, tile, h)
                dve.wait_ge(s_scored, u + 1)
                leaky = nc.vector.scalar_tensor_tensor(buf[:, 0:wide], buf[:, 0:wide], ALPHA[l], buf[:, 0:wide],
                                                       ALU.mult, ALU.max)
                if l != 2:
                    leaky.then_inc(s_leaky, 1)
                    return
                leaky.then_inc(s_counted, 1)
                dve.wait_ge(s_counted, t + 1)
                if c.dense:
                    for g in range(c.groups):
                        nc.vector.tensor_scalar(valid[:, 0:512], buf[:, g * 512:(g + 1) * 512], LOW, 0.0,
                                                ALU.is_gt, ALU.add, accum_out=group_max[:, 1, g:g + 1])\
                            .then_inc(s_counted_part, 1)
                        dve.wait_ge(s_counted_part, t * c.groups + (g + 1))
                    nc.vector.tensor_reduce(st[:, p, COUNT, 0:1], group_max[:, 1, 0:c.groups], AX, ALU.add)\
                        .then_inc(s_leaky, 1)
                else:
                    nc.vector.tensor_scalar(valid[:, 0:wide], buf[:, 0:wide], LOW, 0.0, ALU.is_gt, ALU.add,
                                            accum_out=st[:, p, COUNT, 0:1]).then_inc(s_leaky, 1)

            def threshold(l, plan, tile, h):
                if l != 2:
                    return
                t, p = tile.t, tile_slot(tile)
                buf = attn_buffer(l, tile, h)[:, 0:tile.cls.chunks * P]
                dve.wait_ge(s_exped, unit_index(l, tile, h) + 1)
                nc.vector.reciprocal(st[:, p, RSUM, 0:1], st[:, p, SUM, 0:1]).then_inc(s_recip, 1)
                dve.wait_ge(s_recip, t + (TILES * 2 + 1))
                nc.vector.tensor_scalar(buf, buf, st[:, p, RSUM, 0:1], None, ALU.mult).then_inc(s_attn, 1)
                dve.wait_ge(s_attn, t + 1)
                nc.vector.scalar_tensor_tensor(buf, buf, THRESHOLD, buf, ALU.is_ge, ALU.mult).then_inc(s_normed, 1)

            def combine(l, plan, tile, h):
                nh = HEADS[l]
                if h < nh - 1:
                    return
                c, u, t = tile.cls, unit_index(l, tile, h), tile.t
                p, n = tile_slot(tile), tile.t + l * TILES
                if l != 2:
                    dve.wait_ge(s_exped, u + 1)
                    nc.vector.reciprocal(st[:, p, RSUM, 0:nh], st[:, p, SUM, 0:nh]).then_inc(s_recip, 1)
                nc.vector.tensor_scalar(st[:, p, VALID, 0:nh], st[:, p, BIGGEST, 0:nh], LOW, None, ALU.is_gt)
                nc.vector.tensor_scalar(st[:, p, EMPTY, 0:nh], st[:, p, BIGGEST, 0:nh], LOW, None, ALU.is_le)\
                    .then_inc(s_scale, 1)
                dve.wait_ge(s_recip, n + 1)
                dve.wait_ge(s_scale, n * 2 + 1)
                if l == 2:
                    nc.vector.scalar_tensor_tensor(st[:, p, KEEP, 0:1], st[:, p, RSUM, 0:1], THRESHOLD,
                                                   st[:, p, COUNT, 0:1], ALU.is_gt, ALU.mult).then_inc(s_fin_a, 1)
                    dve.wait_ge(s_fin_a, t + 1)
                    nc.vector.tensor_tensor(st[:, p, SCALE, 0:1], st[:, p, VALID, 0:1], st[:, p, KEEP, 0:1], ALU.mult)\
                        .then_inc(s_scale, 1)
                else:
                    nc.vector.tensor_tensor(st[:, p, SCALE, 0:nh], st[:, p, VALID, 0:nh], st[:, p, RSUM, 0:nh], ALU.mult)\
                        .then_inc(s_scale, 1)
                dve.wait_ge(s_scale, n * 2 + 2)
                dve.wait_ge(s_agg_group, group_index(l, plan, tile, h, c.groups - 1) + 1)
                if due(n):
                    dve.wait_ge(s_x_done, n)
                ag, xt = AG[tile_parity(tile)][:, :], xs[:, t, :]
                scale, empty = st[:, p, SCALE, 0:nh], st[:, p, EMPTY, 0:nh]
                if l < 2:
                    nc.vector.scalar_tensor_tensor(y[:, :], ag, scale, xt, ALU.mult, ALU.add).then_inc(s_fin_b, 1)
                    dve.wait_ge(s_fin_b, n + 1)
                    nc.vector.scalar_tensor_tensor(xt, hbar[:, :], empty, y[:, :], ALU.mult, ALU.add)\
                        .then_inc(s_x_done, 1)
                    return
                m = t + (l - 2) * TILES
                if l == 2:
                    nc.vector.scalar_tensor_tensor(y[:, :], ag, scale, hs[:, t, 0:F], ALU.mult, ALU.add)\
                        .then_inc(s_fin_y, 1)
                else:
                    by_head = ag.rearrange("p (h d) -> p h d", h=nh)
                    hb = hbar[:, :].rearrange("p (h d) -> p h d", h=nh)
                    y3, y23 = (a[:, :].rearrange("p (h d) -> p h d", h=nh) for a in (y, y2))
                    nc.vector.tensor_tensor(y3, by_head, scale.unsqueeze(2).broadcast_to([P, nh, F // nh]), ALU.mult)
                    nc.vector.tensor_tensor(y23, hb, empty.unsqueeze(2).broadcast_to([P, nh, F // nh]), ALU.mult)\
                        .then_inc(s_fin_b, 1)
                    dve.wait_ge(s_fin_b, t + (2 * TILES + 1))
                    nc.vector.tensor_tensor(y[:, :], y[:, :], y2[:, :], ALU.add).then_inc(s_fin_y, 1)
                dve.wait_ge(s_fin_y, m + 1)
                nc.vector.tensor_scalar(neg[:, :], y[:, :], 0.0, None, ALU.min).then_inc(s_neg, 1)

            def elu(l, plan, tile, h):
                if l < 2 or h < HEADS[l] - 1:
                    return
                m, xt = tile.t + (l - 2) * TILES, xs[:, tile.t, :]
                dve.wait_ge(s_exp_neg, m + 1)
                nc.vector.scalar_tensor_tensor(y2[:, :], y[:, :], 0.0, exp_neg[:, :], ALU.max, ALU.add)\
                    .then_inc(s_elu, 1)
                dve.wait_ge(s_elu, m + 1)
                nc.vector.scalar_tensor_tensor(xt, y2[:, :], -1.0, xt, ALU.add, ALU.add).then_inc(s_x_done, 1)

            dve.wait_ge(s_flag, 1)
            many = dve.value_load(over_int[0:1, 0:1])
            with dve.If(many < 1):
                for l in range(LAYERS):
                    soon, later, last_lag = lags(l)
                    if soon:
                        stages = [(soon, leaky_relu), (0, front), (last_lag, combine), (last_lag, elu)]
                    else:
                        stages = [(later, threshold), (0, front), (last_lag, combine), (soon, leaky_relu), (last_lag, elu)]
                    node_work = [(0, 2, node_keep), (1, 1, node_stats), (2, 1, node_normal)]

                    def quad_work(tiles, quad, back_tiles):
                        if tiles[0].cls.dense:
                            run_dense(l, SPARSE, [(0, front), (1, leaky_relu), (2, threshold), (3, combine), (4, elu)],
                                      tiles.pop(0))
                        run_quad(l, stages, node_parts(dve, l + 1, node_work), tiles, back_tiles, quad)
                    last = over_plan(dve, SPARSE, quad_work)
                    run_rest(l, stages, last)
                    if l < 3:
                        node_keep(dve, l + 1, TILES // 4 - 2)
                        node_stats(dve, l + 1, TILES // 4 - 1)
                        node_normal(dve, l + 1, TILES // 4 - 1)
                        node_keep(dve, l + 1, TILES // 4 - 1)
                        mean_begin(dve, l + 1)
                        mean_keep(dve, l + 1)
                dve.nop()
            with dve.Else():
                for l in range(LAYERS):
                    stages = [(0, front), (1, leaky_relu), (2, threshold), (3, combine), (4, elu)]
                    over_plan(dve, DENSE, lambda tiles, quad, back: run_dense(l, DENSE, stages, tiles[0]))
                    if l < 3:
                        def node_all(quad):
                            node_stats(dve, l + 1, quad)
                            node_normal(dve, l + 1, quad)
                            node_keep(dve, l + 1, quad)
                        over_quads(dve, node_all)
                        mean_begin(dve, l + 1)
                        mean_keep(dve, l + 1)
                dve.nop()


_INS = ["x", "adj", "L0_gnn_W", "L0_gnn_a", "L1_gnn_W", "L1_gnn_a", "L2_gnn_W", "L2_gnn_a", "L3_gnn_W", "L3_gnn_a"]
FORCE = False


def kernel(**inputs):
    import numpy as _np
    import concourse.bacc as _bacc
    from concourse import mybir as _mybir
    from concourse.bass_utils import run_bass_kernel_spmd as _run

    nc = _bacc.Bacc("TRN2", target_bir_lowering=False, num_devices=1)
    arrays, args = {}, []
    for name in _INS:
        a = _np.ascontiguousarray(inputs[name])
        arrays[f"in_{name}"] = a
        args.append(nc.dram_tensor(f"in_{name}", a.shape, _mybir.dt.from_np(a.dtype), kind="ExternalInput").ap())
    args.append(nc.dram_tensor("out_x", (8192, 128), _mybir.dt.float32, kind="ExternalOutput").ap())
    gat_kernel(nc, *args)
    r = _run(nc, [arrays], core_ids=[0])
    return r.results[0]["out_x"]
```

```python
from contextlib import ExitStack

import concourse.bass as bass
from concourse import mybir
from concourse.alu_op_type import AluOpType as ALU

FP32 = mybir.dt.float32
BF16 = mybir.dt.bfloat16
I32 = mybir.dt.int32
U32 = mybir.dt.uint32
ACT = mybir.ActivationFunctionType
AX = mybir.AxisListType.X

P = 128
N = 8192
F = 128
TILES = N // P
LAYERS = 4
ALPHA = [0.2, 0.01, 0.2, 0.2]
HEADS = [1, 1, 1, 4]
THRESHOLD = 1e-4
UNIT = float(2.0 ** 83)
LOW = -float(2.0 ** 60)
FLOOR = -3.0e38
EPS = 1e-5
SHIFT = 32
BANK = 4
MAXR = 4


class TileClass:

    def __init__(self, t0, count, runs, rounds, chunks):
        self.t0, self.count, self.runs, self.rounds, self.chunks = t0, count, runs, rounds, chunks
        self.groups = -(-chunks // BANK)
        self.dense = chunks == TILES


class Tile:

    def __init__(self, cls, k, off, quad=None):
        self.cls, self.k, self.off, self.quad = cls, k, off, quad
        self.t = k + cls.t0
        self.slot = (cls.t0 + off) % 4
        self.par = self.slot % 2


DENSE0 = TileClass(0, 1, 0, 0, TILES)
SPARSE = [
    DENSE0,
    TileClass(1, 1, 16, 4, 15),
    TileClass(2, 2, 16, 4, 12),
    TileClass(4, 4, 8, 3, 9),
    TileClass(8, 8, 8, 3, 7),
    TileClass(16, 16, 8, 2, 5),
    TileClass(32, 12, 8, 2, 4),
    TileClass(44, 20, 8, 2, 3),
]
DENSE = [TileClass(0, TILES, 0, 0, TILES)]
SLOTS = 15
CHUNKS = sum(c.count * c.chunks for c in SPARSE[1:])


def run_places(runs):
    return [b + 8 * i for i, b in enumerate(run_bounds(runs)[:-1])]


def run_bounds(runs):
    b = [0]
    for i in range(1, runs):
        b.append(max(int(round(N * (i / runs) ** 2 / 32)) * 32, b[-1] + 32))
    return b + [N]


def before(plan, f, tile):
    total = sum(f(c) * c.count for c in plan if c.t0 < tile.cls.t0)
    return total + tile.k * f(tile.cls)


def before_parity(plan, f, tile):
    total = sum(f(c) * c.count for c in plan if c.t0 < tile.cls.t0)
    return (total + tile.off * f(tile.cls)) % 2


def same_slot(plan, f, tile):
    total = sum(f(c) for c in plan if not c.dense and c.t0 < tile.cls.t0
                for k in range(c.count) if (c.t0 + k) % 4 == tile.slot)
    if tile.cls.count < 4:
        return total + f(tile.cls)
    quad = tile.quad
    return total + quad * f(tile.cls) + f(tile.cls)


def same_parity(tile):
    if tile.cls.count < 4:
        return (tile.t + 1) // 2 if tile.par else tile.t // 2
    t = tile.cls.t0 + tile.off % 4
    return tile.quad * 2 + ((t + 1) // 2 if tile.par else t // 2)


def gat_kernel(nc, x, adj, W0, a0, W1, a1, W2, a2, W3, a3, out, force_dense=False):
    Ws, As = [W0, W1, W2, W3], [a0, a1, a2, a3]
    tables = [nc.dram_tensor(f"table{l}", [N, F + HEADS[l]], FP32).ap() for l in range(LAYERS)]
    ctx = ExitStack()
    with ctx:
        def sb(name, shape, dt):
            return ctx.enter_context(nc.sbuf_tensor(name, shape, dt))

        def pb(name, shape, dt=FP32):
            return ctx.enter_context(nc.psum_tensor(name, shape, dt))

        def sem(name):
            return ctx.enter_context(nc.semaphore(name))

        adj_sb = sb("adj_sb", [P, 2 * N], I32)
        ring = adj_sb[:, N:2 * N].bitcast(FP32)
        xs = sb("xs", [P, TILES, F], FP32)
        hs = sb("hs", [P, TILES, F + 8], FP32)
        scores = sb("scores", [P, N + P], FP32)
        flags = scores[:, :].bitcast(BF16)
        mask = sb("mask", [P, 2, SLOTS * P], BF16)

        onehot = sb("onehot", [P, 2, SHIFT + SLOTS * P], BF16)
        valid = onehot[:, :, :].rearrange("p a b -> p (a b)")
        slot_numbers = sb("slot_numbers", [P, SHIFT + SLOTS * P], FP32)
        columns = sb("columns", [P, CHUNKS], U32)
        column_step = sb("column_step", [P, 4, SLOTS], U32)
        attn_t = sb("attn_t", [P, 2, 512], FP32)
        z = sb("z", [P, 4, F], FP32)
        z_t = sb("z_t", [P, 4 * P], FP32)
        wext = sb("wext", [P, LAYERS, F + 8], FP32)
        a_sb = sb("a_sb", [P, LAYERS, 8], FP32)
        ident = sb("ident", [P, P], FP32)
        before_row = sb("before_row", [P, P], FP32)
        ones = sb("ones", [P, P], FP32)
        z_sum = sb("z_sum", [P, 1], FP32)
        z_total = sb("z_total", [P, 2], FP32)
        hbar = sb("hbar", [P, F], FP32)
        base = sb("base", [P, 26, 8], FP32)
        first = sb("first", [P, TILES], FP32)
        end = sb("end", [P, TILES], FP32)
        over = sb("over", [P, TILES, 3], FP32)
        inside = sb("inside", [P, 16, 8], FP32)
        where = sb("where", [P, 2, 16, 8], U32)
        keys = sb("keys", [P, 16, 8], FP32)
        picked = sb("picked", [P, 2, 8 * MAXR], FP32)
        is_key = sb("is_key", [P, 8 * MAXR], FP32)
        parts = sb("parts", [P, 2, 8 * MAXR, 2], BF16)
        deg = sb("deg", [P, 2], FP32)
        first_step = sb("first_step", [P, 2], FP32)
        listed = sb("listed", [P, SLOTS], FP32)
        over_sum = sb("over_sum", [P, 1], FP32)
        over_int = sb("over_int", [P, 1], I32)
        group_max = sb("group_max", [P, 4, TILES // BANK], FP32)
        st = sb("st", [P, 4, 12, 4], FP32)
        stats = sb("stats", [P, 4, 6], FP32)
        mv = sb("mv", [P, 4, 2], FP32)
        logv = sb("logv", [P, 4], FP32)
        rstd = sb("rstd", [P, 4], FP32)
        eps = sb("eps", [P, 1], FP32)
        minus_low = sb("minus_low", [P, 1], FP32)
        row_sum = sb("row_sum", [P, 4], FP32)
        row_figures = sb("row_figures", [P, 2, 8], FP32)
        y = sb("y", [P, F], FP32)
        y2 = sb("y2", [P, F], FP32)
        neg = sb("neg", [P, F], FP32)
        exp_neg = sb("exp_neg", [P, F], FP32)

        D = [pb("D0", [P, 512]), pb("D1", [P, 512])]
        PT = [pb("PT0", [P, 512]), pb("PT1", [P, 512])]
        AG = [pb("AG0", [P, F + 4]), pb("AG1", [P, F + 4])]
        ZT = pb("ZT", [P, 512])
        HN = pb("HN", [P, 512])

        owner = [scores[:, i * SLOTS * P:(i + 1) * SLOTS * P] for i in range(2)]
        owner_t = [scores[:, i * SLOTS * P:(i + 1) * SLOTS * P] for i in range(2, 4)]
        edge = [keys, inside]
        spread = [HN, ZT]

        BIGGEST, Q, NEGMAX, SUM, RSUM, VALID, SCALE, EMPTY, COUNT, KEEP, LEAST, VALIDS = range(12)

        s_w_loaded = sem("s_w_loaded")
        s_x_loaded = sem("s_x_loaded")
        s_consts = sem("s_consts")
        s_base_fill = sem("s_base_fill")
        s_w_t = sem("s_w_t")
        s_w_t_sb = sem("s_w_t_sb")
        s_wa = sem("s_wa")
        s_wext = sem("s_wext")
        s_flagged = sem("s_flagged")
        s_inside = sem("s_inside")
        s_searched = sem("s_searched")
        s_keys = sem("s_keys")
        s_picks = sem("s_picks")
        s_deg = sem("s_deg")
        s_parts = sem("s_parts")
        s_row_starts = sem("s_row_starts")
        s_first_step = sem("s_first_step")
        s_starts_read = sem("s_starts_read")
        s_onehot = sem("s_onehot")
        s_lists = sem("s_lists")
        s_listed = sem("s_listed")
        s_columns = sem("s_columns")
        s_over = sem("s_over")
        s_over_all = sem("s_over_all")
        s_flag = sem("s_flag")
        s_adj_tile = sem("s_adj_tile")
        s_adj_tile_mask = sem("s_adj_tile_mask")
        s_step_copied = sem("s_step_copied")
        s_mask_half = sem("s_mask_half")
        s_mask = sem("s_mask")
        s_dbcast = sem("s_dbcast")
        s_dscore = sem("s_dscore")
        s_biggest = sem("s_biggest")
        s_q = sem("s_q")
        s_negmax = sem("s_negmax")
        s_scored = sem("s_scored")
        s_leaky = sem("s_leaky")
        s_scored_part = sem("s_scored_part")
        s_leaky_part = sem("s_leaky_part")
        s_exped_part = sem("s_exped_part")
        s_dense_sum = sem("s_dense_sum")
        s_compared = sem("s_compared")
        s_counted = sem("s_counted")
        s_exped = sem("s_exped")
        s_normed = sem("s_normed")
        s_attn = sem("s_attn")
        s_pt = sem("s_pt")
        s_pt_sb = sem("s_pt_sb")
        s_agg_group = sem("s_agg_group")
        s_recip = sem("s_recip")
        s_scale = sem("s_scale")
        s_fin_a = sem("s_fin_a")
        s_fin_b = sem("s_fin_b")
        s_fin_y = sem("s_fin_y")
        s_neg = sem("s_neg")
        s_exp_neg = sem("s_exp_neg")
        s_elu = sem("s_elu")
        s_x_done = sem("s_x_done")
        s_bn = sem("s_bn")
        s_mv = sem("s_mv")
        s_logv = sem("s_logv")
        s_rstd = sem("s_rstd")
        s_z = sem("s_z")
        s_zt = sem("s_zt")
        s_z_t = sem("s_z_t")
        s_hn = sem("s_hn")
        s_h_copied = sem("s_h_copied")
        s_hsum = sem("s_hsum")
        s_hs_low = sem("s_hs_low")
        s_h_sb = sem("s_h_sb")
        s_z_added = sem("s_z_added")
        s_z_mean = sem("s_z_mean")
        s_mean = sem("s_mean")
        s_hbar = sem("s_hbar")
        s_table = sem("s_table")
        s_tile_biggest = sem("s_tile_biggest")
        s_tile_q = sem("s_tile_q")
        s_owner = sem("s_owner")
        s_row_figures = sem("s_row_figures")
        s_spread = sem("s_spread")
        s_turned = sem("s_turned")
        s_owner_t = sem("s_owner_t")
        s_edge_step = sem("s_edge_step")
        s_edge = sem("s_edge")
        s_edge_exp = sem("s_edge_exp")
        s_weighted = sem("s_weighted")
        s_summed = sem("s_summed")
        s_sum_kept = sem("s_sum_kept")
        s_out = sem("s_out")
        s_adj_loaded = [sem(f"s_adj_loaded{i}") for i in range(2)]
        s_gathered = [sem(f"s_gathered{i}") for i in range(4)]

        block = ctx.enter_context(nc.Block())

        def rows_of(tile):
            at = tile.slot * SLOTS * (F + 4)
            return ring[:, at:at + tile.cls.chunks * (F + 4)].rearrange("p (c w) -> p c w", w=F + 4)

        def count_pieces(tile):
            return 4 if tile.cls.dense else 1

        def turn_index(tile, g):
            return before(SPARSE, lambda c: 0 if c.dense else c.groups, tile) + g

        def turn_parity(tile, g):
            return (before_parity(SPARSE, lambda c: 0 if c.dense else c.groups, tile) + g) % 2

        def run_quad(l, stages, node, tiles, back_tiles, quad):
            units = [(tile, 0) for tile in tiles]
            behind = [(tile, 0) for tile in back_tiles]
            behind = [None] * (4 - len(behind)) + behind
            for j in range(len(units)):
                for lag, stage in stages:
                    if isinstance(lag, tuple):
                        stage(l, *((behind + units)[4 + j - k] for k in lag))
                        continue
                    unit = (behind + units)[4 + j - lag]
                    if unit:
                        stage(l, SPARSE, *unit)
                node(j, quad)

        def run_rest(l, stages, back_tiles):
            units = [(tile, 0) for tile in back_tiles]
            for j in range(4):
                for lag, stage in stages:
                    if isinstance(lag, tuple):
                        stage(l, *(units[4 + j - k] if k > j else None for k in lag))
                    elif lag > j:
                        stage(l, SPARSE, *units[4 + j - lag])

        def dense_unit(l, plan, tile, h):
            return unit_index(l, tile, h) if plan is DENSE else sum(HEADS[:l]) + h

        def dense_sums(l, plan, tile):
            layers = l - (l > 2)
            return tile.t + layers * TILES if plan is DENSE else layers

        def dense_part(l, plan, tile, h, i):
            if plan is DENSE:
                return tile.t * (3 * HEADS[l]) + (TILES * 3 * sum(HEADS[k] for k in range(l) if k != 2) + h * 3 + i)
            return 3 * sum(HEADS[k] for k in range(l) if k != 2) + h * 3 + i

        def layer_units(l):
            return TILES * sum(HEADS[:l])

        def unit_index(l, tile, h):
            return tile.t * HEADS[l] + (layer_units(l) + h)

        def group_base(l, plan):
            return sum(c.count * c.groups for c in plan) * sum(HEADS[:l])

        def group_index(l, plan, tile, h, g):
            return before(plan, lambda c: c.groups, tile) * HEADS[l] + (
                group_base(l, plan) + h * tile.cls.groups + g)

        def group_parity(l, plan, tile, h, g):
            n = before_parity(plan, lambda c: c.groups, tile) * HEADS[l]
            return (n + group_base(l, plan) + h * tile.cls.groups + g) % 2

        def dense_mask_count(l, plan, tile, h, g):
            per_head = TILES // BANK
            per_layer = TILES if plan is DENSE else 1
            return tile.t * (HEADS[l] * per_head) + (per_layer * per_head * sum(HEADS[:l]) + h * per_head + g + 1)

        def bank_free(n, g, tile):
            return n if tile.cls.dense and g == 0 else n - 1

        def unit_slot(l, tile, h):
            return 0 if tile.cls.dense else h if HEADS[l] > 1 else tile.slot

        def tile_slot(tile):
            return 0 if tile.cls.dense else tile.slot

        def tile_parity(tile):
            return 0 if tile.cls.dense else tile.par

        def attn_buffer(l, tile, h):
            return scores[:, unit_slot(l, tile, h) * SLOTS * P:]

        def groups_freed(l, plan, tile, h):
            start = group_index(l, plan, tile, h, 0)
            if tile.cls.dense:
                return start
            if tile.cls.t0 < 4:
                return max(start - 3 * tile.cls.groups, group_base(l, plan) + plan[0].groups * HEADS[l])
            return start - 3 * tile.cls.groups

        def features(l, tile, c, lo, hi):
            if tile.cls.dense:
                return hs[:, c, lo:hi]
            at = tile.slot * SLOTS * (F + 4) + c * (F + HEADS[l])
            return ring[:, at + lo:at + hi]

        def over_plan(eng, plan, body):
            if plan is DENSE:
                body([Tile(plan[0], 0, 0)], None, [])
                with eng.Fori(1, TILES) as k:
                    body([Tile(plan[0], k, 0)], None, [])
                return
            tiles = [Tile(c, k, k) for c in plan[:3] for k in range(c.count)]
            body(tiles, 0, [])
            for c in plan[3:]:
                tiles, back = [Tile(c, k, k, 0) for k in range(4)], tiles
                body(tiles, c.t0 // 4, back)
                if c.count > 4:
                    with eng.Fori(1, c.count // 4) as quad:
                        body([Tile(c, quad * 4 + k, k, quad) for k in range(4)], quad + c.t0 // 4,
                             [Tile(c, quad * 4 + (k - 4), k - 4, None) for k in range(4)])
                tiles = [Tile(c, c.count - 4 + k, c.count - 4 + k, c.count // 4 - 1) for k in range(4)]
            return tiles

        def over_quads(eng, body):
            body(0)
            with eng.Fori(1, TILES // 4) as quad:
                body(quad)

        def sparse_tiles(eng, body):
            def without_dense(tiles, quad, back):
                body([t for t in tiles if not t.cls.dense], quad, [t for t in back if not t.cls.dense])
            return over_plan(eng, SPARSE, without_dense)

        def due(value):
            return not isinstance(value, int) or value > 0

        @block.sync
        def _(sp):
            for l in range(LAYERS):
                sp.dma_start(wext[:, l, 0:F], Ws[l]).then_inc(s_w_loaded, 16)
            sp.wait_ge(s_consts, 1)
            for l in range(3):
                sp.dma_start(a_sb[:, l, 0:1], As[l][F:2 * F, :]).then_inc(s_w_loaded, 16)
                sp.dma_start(a_sb[:, l, 1:2], As[l][0:F, :]).then_inc(s_w_loaded, 16)
            for h in range(4):
                for side in range(2):
                    sp.dma_start(a_sb[32 * h:32 * h + 32, 3, 4 * side + h:4 * side + h + 1],
                                 As[3][0, h, 32 * (1 - side):32 * (1 - side) + 32]
                                 .rearrange("(d one) -> d one", one=1)).then_inc(s_w_loaded, 16)
            sp.dma_start(xs[:, :, :], x.rearrange("(t p) f -> p t f", p=P)).then_inc(s_x_loaded, 16)

            def load_rows(tiles, quad, back):
                for tile in tiles:
                    if due(tile.t - 2):
                        sp.wait_ge(s_flagged, tile.t - 2)
                    sp.nop(nofuse=True)
                    sp.dma_start(adj_sb[:, tile.par * N:(tile.par + 1) * N],
                                 adj[bass.ds(tile.t * P, P), :]).then_inc(s_adj_loaded[tile.par], 16)

            sparse_tiles(sp, load_rows)
            sp.wait_ge(s_flagged, TILES - 1)
            sp.dma_start(adj_sb[:, 0:N], adj[0:P, :]).then_inc(s_adj_tile, 16)

            def save_table(l, quad):
                sp.wait_ge(s_h_sb, quad + (l * (TILES // 4) + 1))
                sp.nop(nofuse=True)
                sp.dma_start(tables[l][bass.ds(quad * (4 * P), 4 * P), :].rearrange("(a p) c -> p a c", p=P),
                             hs[:, bass.ds(quad * 4, 4), 0:F + HEADS[l]]).then_inc(s_table, 16)

            def save_x(tile):
                sp.wait_ge(s_x_done, tile.t + 3 * TILES + 1)
                sp.nop(nofuse=True)
                sp.dma_start(out[bass.ds(tile.t * P, P), :], xs[:, tile.t, :]).then_inc(s_out, 16)

            sp.wait_ge(s_flag, 1)
            many = sp.value_load(over_int[0:1, 0:1])
            with sp.If(many < 1):
                over_quads(sp, lambda quad: save_table(0, quad))
                for l in range(LAYERS):
                    if l < 3:
                        over_plan(sp, SPARSE, lambda tiles, quad, back: save_table(l + 1, quad))
                    else:
                        over_plan(sp, SPARSE, lambda tiles, quad, back: [save_x(tile) for tile in tiles])
                sp.nop()
            with sp.Else():
                for l in range(LAYERS):
                    def dense_rows(tiles, quad, back):
                        tile = tiles[0]
                        n = tile.t + l * TILES
                        sp.wait_ge(s_adj_tile, (n + 1) * 16)
                        sp.nop(nofuse=True)
                        if due(tile.t * (16 * HEADS[l]) + l * (TILES * 16)):
                            sp.wait_ge(s_adj_tile_mask, tile.t * (16 * HEADS[l]) + l * (TILES * 16))
                        sp.nop(nofuse=True)
                        sp.dma_start(adj_sb[:, 0:N], adj[bass.ds(tile.t * P, P), :]).then_inc(s_adj_tile, 16)
                        if l == 3:
                            save_x(tile)
                    over_plan(sp, DENSE, dense_rows)
                sp.nop()
            sp.wait_ge(s_out, 16 * TILES)

        @block.gpsimd
        def _(pool):
            pool.memset(a_sb[:, :, :], 0.0).then_inc(s_consts, 1)
            pool.memset(ident[:, :], 0.0).then_inc(s_consts, 1)
            pool.memset(before_row[:, :], 1.0).then_inc(s_consts, 1)
            pool.memset(ones[:, :], 1.0).then_inc(s_consts, 1)
            pool.memset(z_total[:, :], 0.0).then_inc(s_consts, 1)
            pool.memset(eps[:, :], EPS).then_inc(s_consts, 1)
            pool.memset(minus_low[:, :], -LOW).then_inc(s_consts, 1)
            pool.memset(over[:, :, :], 0.0).then_inc(s_consts, 1)
            pool.iota(slot_numbers[:, :], pattern=[[1, SHIFT + SLOTS * P]], base=-SHIFT, channel_multiplier=0,
                      allow_small_or_imprecise_dtypes=True).then_inc(s_consts, 1)
            at = 0
            for runs in (8, 16):
                for b in run_bounds(runs):
                    pool.memset(base[:, at, :], float(b + 1)).then_inc(s_base_fill, 1)
                    at += 1
            pool.wait_ge(s_consts, 9)
            pool.affine_select(out=ident[:, :], in_=ident[:, :], compare_op=ALU.not_equal, fill=1.0,
                               base=0, pattern=[[-1, P]], channel_multiplier=1).then_inc(s_consts, 1)
            pool.affine_select(out=before_row[:, :], in_=before_row[:, :], compare_op=ALU.is_gt, fill=0.0,
                               base=0, pattern=[[1, P]], channel_multiplier=-1).then_inc(s_consts, 1)
            pool.tensor_scalar(slot_numbers[:, :], slot_numbers[:, :], UNIT, None, ALU.mult).then_inc(s_consts, 1)


            def pack(tiles):
                for tile in tiles:
                    c, t, p = tile.cls, tile.t, tile.par
                    n = 8 * c.rounds
                    pool.wait_ge(s_deg, t)
                    if due(t - 2):
                        pool.wait_ge(s_lists, t - 2)
                    pool.nop(nofuse=True)
                    pool.tensor_copy(parts[:, p, 0:n, 0], picked[:, p, 0:n]).then_inc(s_parts, 1)
                    pool.wait_ge(s_parts, t * 2 - 1)
                    pool.tensor_tensor(parts[:, p, 0:n, 1], picked[:, p, 0:n], parts[:, p, 0:n, 0],
                                       ALU.subtract).then_inc(s_parts, 1)
                    wide = SHIFT + c.chunks * P
                    pool.wait_ge(s_first_step, t)
                    pool.nop(nofuse=True)
                    pool.tensor_scalar(onehot[:, p, 0:wide], slot_numbers[:, 0:wide], first_step[:, p:p + 1], None,
                                       ALU.is_equal).then_inc(s_onehot, 1)
            pool.wait_ge(s_consts, 12)
            sparse_tiles(pool, lambda tiles, quad, back: pack(tiles))

            pool.wait_ge(s_flag, 1)
            many = pool.value_load(over_int[0:1, 0:1])
            with pool.If(many < 1):
                for l in range(LAYERS):
                    pool.wait_ge(s_table, 16 * (l + 1) * (TILES // 4))

                    def gather(tiles, quad, back):
                        for tile in tiles:
                            if tile.cls.dense:
                                continue
                            c = tile.cls
                            if tile.cls.t0 >= 4 and HEADS[l] > 1:
                                if due(tile.t - 4):
                                    pool.wait_ge(s_summed, tile.t - 4)
                            elif tile.cls.t0 >= 4:
                                pool.wait_ge(s_agg_group, group_index(l, SPARSE, tile, 0, -3 * HEADS[l] * c.groups))
                            else:
                                if due(group_base(l, SPARSE)):
                                    pool.wait_ge(s_agg_group, group_base(l, SPARSE))
                            at = before(SPARSE, lambda k: 0 if k.dense else k.chunks, tile)
                            pool.tensor_copy(column_step[:, tile.slot, 0:c.chunks], columns[:, bass.ds(at, c.chunks)])\
                                .then_inc(s_step_copied, 1)
                            pool.wait_ge(s_step_copied, tile.t + l * (TILES - 1))
                            pool.nop(nofuse=True)
                            for i in range(c.chunks):
                                pool.indirect_dma_start(
                                    out=features(l, tile, i, 0, F + HEADS[l]), out_offset=None, in_=tables[l],
                                    in_offset=bass.IndirectOffsetOnAxis(ap=column_step[:, tile.slot, i:i + 1], axis=0))\
                                    .then_inc(s_gathered[tile.slot], 16)
                    over_plan(pool, SPARSE, gather)
                pool.nop()
            with pool.Else():
                pool.nop()

        def node_stats(dve, l, quad):
            n = quad + l * (TILES // 4)
            if l == 0:
                dve.wait_ge(s_x_loaded, 16)
            else:
                dve.wait_ge(s_x_done, (n - (TILES // 4)) * 4 + 4)
            if due(n):
                dve.wait_ge(s_z, n)
            for i in range(4):
                op = nc.vector.bn_stats(stats[:, i, :], xs[:, quad * 4 + i, :])
            op.then_inc(s_bn, 1)
            dve.wait_ge(s_bn, n + 1)
            dve.nop(nofuse=True)
            for i in range(4):
                op = nc.vector.bn_aggr(mv[:, i, :], stats[:, i, :])
            op.then_inc(s_mv, 1)

        def node_rstd(act, l, quad):
            n = quad + l * (TILES // 4)
            act.wait_ge(s_mv, n + 1)
            if due(n):
                act.wait_ge(s_z, n)
            nc.scalar.activation(logv[:, :], mv[:, :, 1], ACT.Ln, bias=eps[:, 0:1]).then_inc(s_logv, 1)
            act.wait_ge(s_logv, n + 1)
            nc.scalar.activation(rstd[:, :], logv[:, :], ACT.Exp, scale=-0.5).then_inc(s_rstd, 1)

        def node_normal(dve, l, quad):
            n = quad + l * (TILES // 4)
            dve.wait_ge(s_rstd, n + 1)
            if due(n):
                dve.wait_ge(s_zt, n)
            for i in range(4):
                op = nc.vector.tensor_scalar(z[:, i, :], xs[:, quad * 4 + i, :], mv[:, i, 0:1], rstd[:, i:i + 1],
                                             ALU.subtract, ALU.mult)
            op.then_inc(s_z, 1)

        def node_transpose(pe, l, quad):
            n = quad + l * (TILES // 4)
            pe.wait_ge(s_z, n + 1)
            if due(n):
                pe.wait_ge(s_h_sb, n)
            for i in range(4):
                op = nc.tensor.transpose(ZT[:, i * P:(i + 1) * P], z[:, i, :], ident[:, :])
            op.then_inc(s_zt, 1)

        def node_relu(act, l, quad):
            n = quad + l * (TILES // 4)
            act.wait_ge(s_zt, n + 1)
            if due(n):
                act.wait_ge(s_hn, n)
                act.wait_ge(s_z_added, n)
            nc.scalar.activation(z_t[:, :], ZT[:, :], ACT.Relu, accum_out=z_sum[:, 0:1]).then_inc(s_z_t, 1)

        def node_product(pe, l, quad):
            n = quad + l * (TILES // 4)
            pe.wait_ge(s_z_t, n + 1)
            if due(l):
                pe.wait_ge(s_hbar, l)
            w = F + 2 * HEADS[l]
            for i in range(4):
                bank = (HN, ZT)[i // 2]
                op = nc.tensor.matmul(bank[:, (i % 2) * w:(i % 2 + 1) * w], z_t[:, i * P:(i + 1) * P],
                                      wext[:, l, 0:w], start=True, stop=True)
            op.then_inc(s_hn, 1)

        def node_keep(dve, l, quad):
            n = quad + l * (TILES // 4)
            w = F + 2 * HEADS[l]
            dve.wait_ge(s_z_t, n + 1)
            if due(n):
                dve.wait_ge(s_z_added, n)
            nc.vector.tensor_tensor(z_total[:, 0:1], z_total[:, 0:1], z_sum[:, 0:1], ALU.add).then_inc(s_z_added, 1)
            dve.wait_ge(s_hn, n + 1)
            for i, bank in enumerate((HN, ZT)):
                op = nc.vector.tensor_copy(hs[:, bass.ds(quad * 4 + 2 * i, 2), 0:w],
                                           bank[:, 0:2 * w].rearrange("p (t c) -> p t c", t=2))
            if l != 2:
                op.then_inc(s_h_sb, 1)
                return
            op.then_inc(s_h_copied, 1)
            for i, bank in enumerate((HN, ZT)):
                op = nc.vector.tensor_reduce(row_sum[:, 2 * i:2 * i + 2],
                                             bank[:, 0:2 * w].rearrange("p (t c) -> p t c", t=2)[:, :, 0:F],
                                             AX, ALU.add)
            op.then_inc(s_hsum, 1)
            dve.wait_ge(s_hsum, quad + 1)
            nc.vector.tensor_scalar(row_sum[:, :], row_sum[:, :], 0.0, -UNIT, ALU.is_equal, ALU.mult).then_inc(s_hs_low, 1)
            dve.wait_ge(s_hs_low, quad + 1)
            dve.wait_ge(s_h_copied, quad + 1)
            nc.vector.tensor_tensor(hs[:, bass.ds(quad * 4, 4), F], hs[:, bass.ds(quad * 4, 4), F], row_sum[:, :],
                                    ALU.add).then_inc(s_h_sb, 1)

        def node_parts(eng, l, parts):
            def node(step, quad):
                for at, back, part in parts:
                    if at == step and (not isinstance(quad, int) or quad >= back):
                        part(eng, l, quad - back)
            return node if l < LAYERS else lambda step, quad: None

        def mean_begin(dve, l):
            dve.wait_ge(s_z_added, (l + 1) * (TILES // 4))
            nc.vector.tensor_scalar(z_total[:, 1:2], z_total[:, 0:1], 1.0 / N, None, ALU.mult).then_inc(s_z_mean, 1)
            dve.wait_ge(s_z_mean, l + 1)
            nc.vector.memset(z_total[:, 0:1], 0.0)

        def mean_product(pe, l):
            pe.wait_ge(s_z_mean, l + 1)
            pe.wait_ge(s_h_sb, (l + 1) * (TILES // 4))
            nc.tensor.matmul(HN[:, 0:F], z_total[:, 1:2].broadcast_to([P, P]), wext[:, l, 0:F],
                             start=True, stop=True).then_inc(s_mean, 1)

        def mean_keep(dve, l):
            dve.wait_ge(s_mean, l + 1)
            nc.vector.tensor_copy(hbar[:, :], HN[:, 0:F]).then_inc(s_hbar, 1)

        @block.tensor
        def _(pe):
            pe.wait_ge(s_consts, 12)
            pe.wait_ge(s_w_loaded, 16 * (LAYERS + 6 + 8))
            for l in range(LAYERS):
                nc.tensor.transpose(PT[0][:, l * P:(l + 1) * P], wext[:, l, 0:F], ident[:, :]).then_inc(s_w_t, 1)
            pe.wait_ge(s_w_t_sb, 1)
            for l in range(LAYERS):
                nh = HEADS[l]
                for side in range(2):
                    at = side * (4 if l == 3 else 1)
                    op = nc.tensor.matmul(PT[1][:, l * 8 + side * nh:l * 8 + (side + 1) * nh],
                                          attn_t[:, 0, l * P:(l + 1) * P], a_sb[:, l, at:at + nh], start=True, stop=True)
            op.then_inc(s_wa, 1)
            pe.wait_ge(s_wext, 1)
            def row_starts(tile):
                pe.wait_ge(s_deg, tile.t)
                if due(tile.t - 1):
                    pe.wait_ge(s_starts_read, tile.t - 1)
                nc.tensor.matmul(D[0][:, 0:1], before_row[:, :], deg[:, tile.par:tile.par + 1],
                                 start=True, stop=True).then_inc(s_row_starts, 1)

            def list_keys(tile):
                pe.wait_ge(s_onehot, tile.t)
                if due(tile.t - 1):
                    pe.wait_ge(s_listed, tile.t - 1)
                n = 8 * tile.cls.rounds
                for c in range(tile.cls.chunks):
                    for k in range(n):
                        at = SHIFT - k + c * P
                        op = nc.tensor.matmul(PT[0][:, 2 * c:2 * c + 2], onehot[:, tile.par, at:at + P],
                                              parts[:, tile.par, k, :], start=k == 0, stop=k == n - 1)
                op.then_inc(s_lists, 1)

            def scan(tiles, quad, back):
                for i, tile in enumerate(tiles):
                    if tile.slot == 3:
                        node_transpose(pe, 0, quad)
                        node_product(pe, 0, quad)
                    row_starts(tile)
                    if i or back:
                        list_keys(([*back, *tiles])[len(back) + i - 1])
            last = sparse_tiles(pe, scan)
            list_keys(last[-1])
            mean_product(pe, 0)
            pe.wait_ge(s_over, 1)
            nc.tensor.matmul(D[1][:, 0:1], ones[:, :], over_sum[:, :], start=True, stop=True).then_inc(s_over_all, 1)

            def front(l, plan, tile, h):
                c = tile.cls
                if not c.dense and h == 0:
                    got = same_slot(plan, lambda k: 16 * k.chunks, tile)
                    whole = sum(16 * k.chunks for k in SPARSE[1:] for i in range(k.count)
                                if (k.t0 + i) % 4 == tile.slot)
                    pe.wait_ge(s_gathered[tile.slot], got + l * whole)
                if c.dense:
                    pe.wait_ge(s_h_sb, (l + 1) * (TILES // 4))
                for g in range(c.groups):
                    front_group(l, plan, tile, h, g)

            def front_group(l, plan, tile, h, g):
                n, par = group_index(l, plan, tile, h, g), group_parity(l, plan, tile, h, g)
                if due(bank_free(n, g, tile)):
                    pe.wait_ge(s_dscore, bank_free(n, g, tile))
                for i in range(min(BANK, tile.cls.chunks - g * BANK)):
                    d = features(l, tile, g * BANK + i, F + h, F + h + 1)
                    op = nc.tensor.transpose(D[par][:, i * P:(i + 1) * P], d.broadcast_to([P, P]), ident[:, :])
                op.then_inc(s_dbcast, 1)

            def turn(l, plan, tile, h, g):
                c, src = tile.cls, attn_buffer(l, tile, h)
                if c.dense and l != 2 and g % 4 == 0:
                    if g < 12:
                        pe.wait_ge(s_exped_part, dense_part(l, plan, tile, h, g // 4) + 1)
                    else:
                        pe.wait_ge(s_exped, unit_index(l, tile, h) + 1)
                n, par = group_index(l, plan, tile, h, g), group_parity(l, plan, tile, h, g)
                if due(bank_free(n, g, tile)):
                    pe.wait_ge(s_pt_sb, bank_free(n, g, tile))
                for i in range(min(BANK, c.chunks - g * BANK)):
                    j = g * BANK + i
                    op = nc.tensor.transpose(PT[par][:, i * P:(i + 1) * P], src[:, j * P:(j + 1) * P], ident[:, :])
                op.then_inc(s_pt, 1)

            def transposes(l, plan, tile, h):
                if l == 2:
                    pe.wait_ge(s_normed, tile.t + 1)
                elif not tile.cls.dense:
                    pe.wait_ge(s_exped, unit_index(l, tile, h) + 1)
                for g in range(min(2, tile.cls.groups)):
                    turn(l, plan, tile, h, g)

            def products(l, plan, tile, h):
                c, u = tile.cls, unit_index(l, tile, h)
                if h == 0:
                    done = tile.t + l * TILES
                    if due(done if c.dense else done - 1):
                        pe.wait_ge(s_x_done, done if c.dense else done - 1)
                wide = F // HEADS[l]

                for g in range(c.groups):
                    n, par = group_index(l, plan, tile, h, g), group_parity(l, plan, tile, h, g)
                    pe.wait_ge(s_pt_sb, n + 1)
                    for i in range(min(BANK, c.chunks - g * BANK)):
                        j = g * BANK + i
                        op = nc.tensor.matmul(AG[tile_parity(tile)][:, h * wide:(h + 1) * wide],
                                              attn_t[:, par, i * P:(i + 1) * P],
                                              features(l, tile, j, h * wide, (h + 1) * wide),
                                              start=j == 0, stop=j == c.chunks - 1)
                    op.then_inc(s_agg_group, 1)
                    if g + 2 < c.groups:
                        turn(l, plan, tile, h, g + 2)
                    if c.dense and h + 1 < HEADS[l]:
                        front_group(l, plan, tile, h + 1, g)

            def dense_tile(l, plan, tile):
                front(l, plan, tile, 0)
                for h in range(HEADS[l]):
                    transposes(l, plan, tile, h)
                    products(l, plan, tile, h)

            def front_heads(l, plan, tile, _):
                for h in range(HEADS[l]):
                    front(l, plan, tile, h)

            def spread_figures(l, plan, tile, _):
                pe.wait_ge(s_row_figures, tile.t)
                for c in range(tile.cls.chunks):
                    op = nc.tensor.matmul(spread[tile.par][:, 8 * c:8 * c + 8], owner[tile.par][:, c * P:(c + 1) * P],
                                          row_figures[:, tile.par, :], start=True, stop=True)
                op.then_inc(s_spread, 1)

            def turn_owner(l, plan, tile, _):
                pe.wait_ge(s_owner, tile.t)
                for g in range(tile.cls.groups):
                    n, par = turn_index(tile, g), turn_parity(tile, g)
                    if due(n - 1):
                        pe.wait_ge(s_owner_t, n - 1)
                    for i in range(min(BANK, tile.cls.chunks - g * BANK)):
                        j = g * BANK + i
                        op = nc.tensor.transpose(PT[par][:, i * P:(i + 1) * P], owner[tile.par][:, j * P:(j + 1) * P],
                                                 ident[:, :])
                    op.then_inc(s_turned, 1)

            def sum_rows(l, plan, tile, _):
                c = tile.cls
                pe.wait_ge(s_weighted, tile.t)
                pe.wait_ge(s_owner_t, turn_index(tile, c.groups))
                pe.wait_ge(s_x_done, tile.t + (l * TILES - 1))
                for j in range(c.chunks):
                    op = nc.tensor.matmul(AG[tile.par][:, :], owner_t[tile.par][:, j * P:(j + 1) * P],
                                          rows_of(tile)[:, j, :], start=j == 0, stop=j == c.chunks - 1)
                op.then_inc(s_summed, 1)

            pe.wait_ge(s_flag, 1)
            many = pe.value_load(over_int[0:1, 0:1])
            with pe.If(many < 1):
                for l in range(LAYERS):
                    stages = [(0, front), (1, transposes), (1, products)]
                    if HEADS[l] > 1:
                        stages = [(1, spread_figures), (0, front_heads), (2, sum_rows), (0, turn_owner)]
                    node_work = [(0, 2, node_transpose), (2, 2, node_product)]

                    def quad_work(tiles, quad, back_tiles):
                        if tiles[0].cls.dense:
                            dense_tile(l, SPARSE, tiles.pop(0))
                            if HEADS[l] > 1:
                                pe.wait_ge(s_hbar, LAYERS)
                                pe.wait_ge(s_x_done, l * TILES + 1)
                        run_quad(l, stages, node_parts(pe, l + 1, node_work), tiles, back_tiles, quad)
                    last = over_plan(pe, SPARSE, quad_work)
                    run_rest(l, stages, last)
                    if l < 3:
                        node_transpose(pe, l + 1, TILES // 4 - 2)
                        node_product(pe, l + 1, TILES // 4 - 2)
                        node_transpose(pe, l + 1, TILES // 4 - 1)
                        node_product(pe, l + 1, TILES // 4 - 1)
                        mean_product(pe, l + 1)
                pe.nop()
            with pe.Else():
                for l in range(LAYERS):
                    over_plan(pe, DENSE, lambda tiles, quad, back: dense_tile(l, DENSE, tiles[0]))
                    if l < 3:
                        def node_both(quad):
                            node_transpose(pe, l + 1, quad)
                            node_product(pe, l + 1, quad)
                        over_quads(pe, node_both)
                        mean_product(pe, l + 1)
                pe.nop()

        @block.scalar
        def _(act):
            act.preload_act_table_set("natural_log_exp_and_others")
            act.wait_ge(s_w_t, LAYERS)
            nc.scalar.activation(attn_t[:, 0, :], PT[0][:, :], ACT.Copy).then_inc(s_w_t_sb, 1)
            act.wait_ge(s_consts, 7)

            def sentinels(runs, p):
                bounds, places = run_bounds(runs), run_places(runs)
                for i in range(runs):
                    at = p * (N + P) + places[i] + bounds[i + 1] - bounds[i]
                    op = nc.scalar.activation(flags[:, at:at + 8], ones[:, 0:8], ACT.Copy)
                return op

            def flag_rows(tiles, quad, back):
                for tile in tiles:
                    c, t, p = tile.cls, tile.t, tile.par
                    bounds, places = run_bounds(c.runs), run_places(c.runs)
                    if due(t - 2):
                        act.wait_ge(s_searched, t - 2)
                    if isinstance(t, int) and (t < 3 or 4 <= t < 6):
                        sentinels(c.runs, p)
                    act.wait_ge(s_adj_loaded[p], same_parity(tile) * 16)
                    for i in range(c.runs):
                        at = p * (N + P) + places[i]
                        op = nc.scalar.activation(flags[:, at:at + bounds[i + 1] - bounds[i]],
                                                  adj_sb[:, p * N + bounds[i]:p * N + bounds[i + 1]], ACT.Sign)
                    op.then_inc(s_flagged, 1)
                    if tile.slot == 2:
                        node_rstd(act, 0, quad)
                    elif tile.slot == 0:
                        node_relu(act, 0, quad - 1)
            sparse_tiles(act, flag_rows)
            node_relu(act, 0, TILES // 4 - 1)

            def shift(l, plan, tile, h):
                c = tile.cls
                buf = attn_buffer(l, tile, h)[:, 0:c.chunks * P]
                act.wait_ge(s_dscore, group_index(l, plan, tile, h, c.groups - 1) + 1)
                row = hs[:, tile.t, F + HEADS[l] + h:F + HEADS[l] + h + 1]
                nc.scalar.activation(buf, buf, ACT.Identity, bias=row).then_inc(s_scored, 1)

            def shift_group(l, plan, tile, h, g):
                buf = scores[:, g * 512:(g + 1) * 512]
                row = hs[:, tile.t, F + HEADS[l] + h:F + HEADS[l] + h + 1]
                act.wait_ge(s_dscore, group_index(l, plan, tile, h, g) + 1)
                act.nop(nofuse=True)
                op = nc.scalar.activation(buf, buf, ACT.Identity, bias=row)
                op.then_inc(s_scored_part if g < tile.cls.groups - 1 else s_scored, 1)

            def exponent(l, plan, tile, h):
                u, p = unit_index(l, tile, h), tile_slot(tile)
                buf = attn_buffer(l, tile, h)[:, 0:tile.cls.chunks * P]
                act.wait_ge(s_leaky, u + 1)
                act.wait_ge(s_negmax, u + 1)
                if l == 2:
                    pieces = count_pieces(tile)
                    wide = tile.cls.chunks * P // pieces
                    for i in range(pieces):
                        done = tile.t * 4 + i if tile.cls.dense else tile.t + 3
                        if due(done):
                            act.wait_ge(s_compared, done)
                        nc.scalar.activation(valid[:, 0:wide], buf[:, i * wide:(i + 1) * wide], ACT.Sign,
                                             bias=minus_low[:, 0:1], accum_out=st[:, p, COUNT, i:i + 1]).then_inc(s_compared, 1)
                    act.wait_ge(s_compared, done + 1)
                if tile.cls.dense and l != 2:
                    for i in range(4):
                        quarter = scores[:, i * (N // 4):(i + 1) * (N // 4)]
                        op = nc.scalar.activation(quarter, quarter, ACT.Exp, bias=st[:, p, NEGMAX, h:h + 1],
                                                  accum_out=group_max[:, 3, 4 * h + i:4 * h + i + 1])
                        op.then_inc(s_exped_part if i < 3 else s_exped, 1)
                    return
                nc.scalar.activation(buf, buf, ACT.Exp, bias=st[:, p, NEGMAX, h:h + 1],
                                     accum_out=st[:, p, SUM, h:h + 1]).then_inc(s_exped, 1)

            def evacuate(l, plan, tile, h):
                for g in range(tile.cls.groups):
                    n, par = group_index(l, plan, tile, h, g), group_parity(l, plan, tile, h, g)
                    wide = min(BANK, tile.cls.chunks - g * BANK) * P
                    act.wait_ge(s_pt, n + 1)
                    if due(bank_free(n, g, tile)):
                        act.wait_ge(s_agg_group, bank_free(n, g, tile))
                    nc.scalar.activation(attn_t[:, par, 0:wide], PT[par][:, 0:wide], ACT.Copy).then_inc(s_pt_sb, 1)
                    if tile.cls.dense and h + 1 < HEADS[l] and g > 0:
                        shift_group(l, plan, tile, h + 1, g - 1)
                if tile.cls.dense and h + 1 < HEADS[l]:
                    shift_group(l, plan, tile, h + 1, tile.cls.groups - 1)

            def negative_exp(l, plan, tile, h):
                if l < 2 or h < HEADS[l] - 1:
                    return
                act.wait_ge(s_neg, tile.t + ((l - 2) * TILES + 1))
                nc.scalar.activation(exp_neg[:, :], neg[:, :], ACT.Exp).then_inc(s_exp_neg, 1)

            def dense_tile(l, plan, tile):
                for g in range(tile.cls.groups):
                    shift_group(l, plan, tile, 0, g)
                for h in range(HEADS[l]):
                    exponent(l, plan, tile, h)
                    evacuate(l, plan, tile, h)
                negative_exp(l, plan, tile, HEADS[l] - 1)

            def edge_exponent(l, plan, tile, _):
                act.wait_ge(s_edge, tile.t)
                nc.scalar.activation(rows_of(tile)[:, :, F:F + 4], edge[tile.par][:, 0:tile.cls.chunks, 0:4], ACT.Exp)\
                    .then_inc(s_edge_exp, 1)

            def tile_negative_exp(l, plan, tile, _):
                negative_exp(l, plan, tile, HEADS[l] - 1)

            def evacuate_owner(l, plan, tile, _):
                if due(tile.t - 2):
                    act.wait_ge(s_summed, tile.t - 2)
                for g in range(tile.cls.groups):
                    n, par = turn_index(tile, g), turn_parity(tile, g)
                    wide = min(BANK, tile.cls.chunks - g * BANK) * P
                    act.wait_ge(s_turned, n + 1)
                    nc.scalar.activation(owner_t[tile.par][:, g * 512:g * 512 + wide], PT[par][:, 0:wide], ACT.Copy)\
                        .then_inc(s_owner_t, 1)

            act.wait_ge(s_flag, 1)
            many = act.value_load(over_int[0:1, 0:1])
            with act.If(many < 1):
                for l in range(LAYERS):
                    stages = [(0, shift), (1, evacuate), (2, negative_exp), (0, exponent)]
                    if HEADS[l] > 1:
                        stages = [(3, tile_negative_exp), (1, edge_exponent), (0, evacuate_owner)]
                    node_work = [(3, 1, node_rstd), (1, 2, node_relu)]

                    def quad_work(tiles, quad, back_tiles):
                        if tiles[0].cls.dense:
                            dense_tile(l, SPARSE, tiles.pop(0))
                            if HEADS[l] > 1:
                                act.wait_ge(s_x_done, l * TILES + 1)
                        run_quad(l, stages, node_parts(act, l + 1, node_work), tiles, back_tiles, quad)
                    last = over_plan(act, SPARSE, quad_work)
                    run_rest(l, stages, last)
                    if l < 3:
                        node_relu(act, l + 1, TILES // 4 - 2)
                        node_rstd(act, l + 1, TILES // 4 - 1)
                        node_relu(act, l + 1, TILES // 4 - 1)
                act.nop()
            with act.Else():
                for l in range(LAYERS):
                    over_plan(act, DENSE, lambda tiles, quad, back: dense_tile(l, DENSE, tiles[0]))
                    if l < 3:
                        def node_both(quad):
                            node_rstd(act, l + 1, quad)
                            node_relu(act, l + 1, quad)
                        over_quads(act, node_both)
                act.nop()

        @block.vector
        def _(dve):
            dve.wait_ge(s_wa, 1)
            for l in range(LAYERS):
                op = nc.vector.tensor_copy(wext[:, l, F:F + 2 * HEADS[l]], PT[1][:, l * 8:l * 8 + 2 * HEADS[l]])
            op.then_inc(s_wext, 1)
            dve.wait_ge(s_consts, 12)
            dve.wait_ge(s_base_fill, 26)

            def keys_of(tile):
                c, t, p = tile.cls, tile.t, tile.par
                at = {8: 0, 16: 9}[c.runs]
                k, v = keys[:, 0:c.runs, :], inside[:, 0:c.runs, :]
                dve.wait_ge(s_searched, t)
                if due(t - 1):
                    dve.wait_ge(s_deg, t - 1)
                nc.vector.tensor_tensor(k, where[:, p, 0:c.runs, :], base[:, at:at + c.runs, :], ALU.add)\
                    .then_inc(s_keys, 1)
                yield
                dve.wait_ge(s_keys, t * 2 - 1)
                nc.vector.tensor_tensor(v, k, base[:, at + 1:at + 1 + c.runs, :], ALU.is_lt).then_inc(s_inside, 1)
                yield
                dve.wait_ge(s_inside, t)
                nc.vector.tensor_tensor(k, k, v, ALU.mult).then_inc(s_keys, 1)
                nc.vector.tensor_reduce(over[:, bass.ds(t, 1), 0:1], inside[:, 0:c.runs, 7], AX, ALU.max)
                yield
                flat = k.rearrange("p r e -> p (r e)")
                done = before(SPARSE, lambda x: max(2 * x.rounds - 1, 0), tile)
                if due(t - 2):
                    dve.wait_ge(s_parts, t * 2 - 4)
                    dve.nop(nofuse=True)
                dve.wait_ge(s_keys, t * 2)
                dve.nop(nofuse=True)
                for i in range(c.rounds):
                    nc.vector.max(picked[:, p, 8 * i:8 * i + 8], flat).then_inc(s_picks, 1)
                    yield
                    dve.wait_ge(s_picks, done + (2 * i + 1))
                    dve.nop(nofuse=True)
                    if i < c.rounds - 1:
                        nc.vector.match_replace(flat, picked[:, p, 8 * i:8 * i + 8], flat, 0.0).then_inc(s_picks, 1)
                        yield
                        dve.wait_ge(s_picks, done + (2 * i + 2))
                        dve.nop(nofuse=True)
                n = 8 * c.rounds
                nc.vector.tensor_copy(over[:, bass.ds(t, 1), 1:2], picked[:, p, n - 1:n])
                nc.vector.tensor_scalar(is_key[:, 0:n], picked[:, p, 0:n], 0.0, 0.0, ALU.is_gt, ALU.add,
                                        accum_out=deg[:, p:p + 1]).then_inc(s_deg, 1)
                yield

            def row_slots(tile):
                c, t, p = tile.cls, tile.t, tile.par
                dve.wait_ge(s_row_starts, t)
                if due(t - 2):
                    dve.wait_ge(s_onehot, t - 2)
                nc.vector.tensor_scalar(first_step[:, p:p + 1], D[0][:, 0:1], UNIT, None, ALU.mult).then_inc(s_first_step, 1)
                nc.vector.tensor_scalar(first[:, bass.ds(t, 1)], D[0][:, 0:1], UNIT, None, ALU.mult)
                nc.vector.tensor_scalar(end[:, bass.ds(t, 1)], D[0][:, 0:1], deg[:, p:p + 1], UNIT, ALU.add, ALU.mult)\
                    .then_inc(s_starts_read, 1)
                dve.wait_ge(s_starts_read, t)
                nc.vector.tensor_scalar(over[:, bass.ds(t, 1), 2:3], end[:, bass.ds(t, 1)], UNIT * P * c.chunks, None, ALU.is_gt)

            def write_list(tile):
                c, t = tile.cls, tile.t
                dve.wait_ge(s_lists, t)
                if due(t - 1):
                    dve.wait_ge(s_columns, t - 1)
                nc.vector.tensor_reduce(listed[:, 0:c.chunks], PT[0][:, 0:2 * c.chunks].rearrange("p (c two) -> p c two", two=2),
                                        AX, ALU.add).then_inc(s_listed, 1)
                dve.wait_ge(s_listed, t)
                at = before(SPARSE, lambda k: 0 if k.dense else k.chunks, tile)
                nc.vector.tensor_scalar(columns[:, bass.ds(at, c.chunks)], listed[:, 0:c.chunks], 1.0, -1.0,
                                        ALU.max, ALU.add).then_inc(s_columns, 1)

            def scan(tiles, quad, back):
                for i, tile in enumerate(tiles):
                    c, t, p = tile.cls, tile.t, tile.par
                    earlier = [*back, *tiles[:i]]
                    bounds, places = run_bounds(c.runs), run_places(c.runs)
                    steps = keys_of(earlier[-1]) if earlier else iter(())
                    if len(earlier) > 1:
                        row_slots(earlier[-2])
                    dve.wait_ge(s_flagged, t)
                    dve.nop(nofuse=True)
                    for run in range(c.runs):
                        at = p * (N + P) + places[run]
                        op = nc.vector.max_index(where[:, p, run, :], ones[:, 0:8],
                                                 flags[:, at:at + bounds[run + 1] - bounds[run] + 8])
                        if run == c.runs - 1:
                            op.then_inc(s_searched, 1)
                        next(steps, None)
                    for _ in steps:
                        pass
                    if len(earlier) > 2:
                        write_list(earlier[-3])
                    if tile.slot == 1:
                        node_stats(dve, 0, quad)
                    elif tile.slot == 3:
                        node_normal(dve, 0, quad)
                    elif tile.slot == 0:
                        node_keep(dve, 0, quad - 1)

            last = sparse_tiles(dve, scan)
            row_slots(last[-2])
            for _ in keys_of(last[-1]):
                pass
            write_list(last[-3])
            row_slots(last[-1])
            node_keep(dve, 0, TILES // 4 - 1)
            write_list(last[-2])
            write_list(last[-1])
            mean_begin(dve, 0)
            mean_keep(dve, 0)
            dve.wait_ge(s_columns, TILES - 1)
            dve.wait_ge(s_starts_read, TILES - 1)
            nc.vector.tensor_reduce(over_sum[:, :], over[:, :, :].rearrange("p t c -> p (t c)"), AX, ALU.max)\
                .then_inc(s_listed, 1)
            dve.wait_ge(s_listed, TILES)
            nc.vector.tensor_scalar(over_sum[:, :], over_sum[:, :], 0.0, 1.0, ALU.is_gt, ALU.mult).then_inc(s_over, 1)
            dve.wait_ge(s_over_all, 1)
            nc.vector.tensor_scalar(over_int[:, :], D[1][:, 0:1], 1.0 if force_dense else 0.0, None, ALU.add)\
                .then_inc(s_flag, 1)

            def mask_slots(l, plan, tile, h):
                wide, n, t = tile.cls.chunks * P, tile.t + l * (TILES - 1), tile.t
                m = mask[:, tile.par, 0:wide]
                numbers = slot_numbers[:, SHIFT:SHIFT + wide]
                nc.vector.tensor_scalar(m, numbers, end[:, bass.ds(t, 1)], -UNIT, ALU.is_ge, ALU.mult).then_inc(s_mask_half, 1)
                if due(n):
                    dve.wait_ge(s_mask_half, n)
                nc.vector.scalar_tensor_tensor(m, numbers, first[:, bass.ds(t, 1)], m, ALU.subtract, ALU.min)\
                    .then_inc(s_mask, 1)
                if due(n):
                    dve.wait_ge(s_mask, n)

            def front(l, plan, tile, h):
                c, u, t = tile.cls, unit_index(l, tile, h), tile.t
                p, up = tile_slot(tile), unit_slot(l, tile, h)
                buf = attn_buffer(l, tile, h)
                wide = c.chunks * P
                if c.dense:
                    if h == 0 and plan is DENSE:
                        dve.wait_ge(s_adj_tile, (t + (l * TILES + 2)) * 16)
                    elif h == 0:
                        dve.wait_ge(s_adj_tile, 16)
                if due(groups_freed(l, plan, tile, h)) and (h == 0 or not c.dense):
                    dve.wait_ge(s_pt, groups_freed(l, plan, tile, h))
                for g in range(c.groups):
                    n, par = group_index(l, plan, tile, h, g), group_parity(l, plan, tile, h, g)
                    cols = min(BANK, c.chunks - g * BANK) * P
                    if c.dense:
                        if h > 0:
                            dve.wait_ge(s_pt, group_index(l, plan, tile, h - 1, g) + 1)
                        m = mask[:, 0, (g % 2) * 512:(g % 2) * 512 + cols]
                        if due(n - 1):
                            dve.wait_ge(s_dscore, n - 1)
                        op = nc.vector.tensor_scalar(m, adj_sb[:, g * 512:g * 512 + cols], 0.0, -UNIT, ALU.is_le, ALU.mult)
                        op.then_inc(s_adj_tile_mask, 1)
                        dve.wait_ge(s_adj_tile_mask, dense_mask_count(l, plan, tile, h, g))
                    else:
                        m = mask[:, tile.par, g * 512:g * 512 + cols]
                    dve.wait_ge(s_dbcast, n + 1)
                    dve.nop(nofuse=True)
                    nc.vector.tensor_tensor_reduce(out=buf[:, g * 512:g * 512 + cols], in0=D[par][:, 0:cols], in1=m,
                                                   scale=1.0, scalar=FLOOR, op0=ALU.add, op1=ALU.max,
                                                   accum_out=group_max[:, up, g:g + 1]).then_inc(s_dscore, 1)
                    if c.dense and g > 0:
                        leaky_group(l, plan, tile, h, g - 1)
                yield
                dve.wait_ge(s_dscore, group_index(l, plan, tile, h, c.groups - 1) + 1)
                biggest = st[:, p, BIGGEST, h:h + 1]
                nc.vector.tensor_reduce(biggest, group_max[:, up, 0:c.groups], AX, ALU.max).then_inc(s_biggest, 1)
                yield
                dve.wait_ge(s_biggest, u + 1)
                row = hs[:, t, F + HEADS[l] + h:F + HEADS[l] + h + 1]
                q = st[:, p, Q, h:h + 1]
                nc.vector.tensor_scalar(q, biggest, row, -1.0, ALU.add, ALU.mult).then_inc(s_q, 1)
                yield
                dve.wait_ge(s_q, u + 1)
                nc.vector.scalar_tensor_tensor(st[:, p, NEGMAX, h:h + 1], q, ALPHA[l], q, ALU.mult, ALU.min)\
                    .then_inc(s_negmax, 1)

            def front_heads(l, plan, tile, _):
                c, t, p, nh, par = tile.cls, tile.t, tile.slot, HEADS[l], tile.par
                wide, n = c.chunks * P, tile.t + l * (TILES - 1)
                mask_slots(l, plan, tile, 0)
                if due(t - 2):
                    dve.wait_ge(s_spread, t - 2)
                nc.vector.tensor_scalar(owner[par][:, 0:wide], mask[:, par, 0:wide], 0.0, None, ALU.is_equal)\
                    .then_inc(s_owner, 1)
                row = hs[:, t, F + nh:F + 2 * nh]
                nc.vector.tensor_copy(row_figures[:, par, 0:nh], row)
                for h in range(nh):
                    for g in range(c.groups):
                        n, bank = group_index(l, plan, tile, h, g), group_parity(l, plan, tile, h, g)
                        cols = min(BANK, c.chunks - g * BANK) * P
                        dve.wait_ge(s_dscore, n - 1)
                        dve.wait_ge(s_dbcast, n + 1)
                        dve.nop(nofuse=True)
                        nc.vector.tensor_tensor_reduce(out=attn_t[:, bank, 0:cols], in0=D[bank][:, 0:cols],
                                                       in1=mask[:, par, g * 512:g * 512 + cols],
                                                       scale=1.0, scalar=FLOOR, op0=ALU.add, op1=ALU.max,
                                                       accum_out=group_max[:, h, g:g + 1]).then_inc(s_dscore, 1)
                        yield
                dve.wait_ge(s_dscore, group_index(l, plan, tile, nh - 1, c.groups - 1) + 1)
                biggest, q = st[:, p, BIGGEST, 0:nh], st[:, p, Q, 0:nh]
                nc.vector.tensor_reduce(biggest, group_max[:, :, 0:c.groups], AX, ALU.max).then_inc(s_tile_biggest, 1)
                yield
                dve.wait_ge(s_tile_biggest, t)
                nc.vector.scalar_tensor_tensor(q, biggest, -1.0, row, ALU.mult, ALU.subtract).then_inc(s_tile_q, 1)
                yield
                dve.wait_ge(s_tile_q, t)
                nc.vector.scalar_tensor_tensor(row_figures[:, par, nh:2 * nh], q, ALPHA[l], q, ALU.mult, ALU.min)\
                    .then_inc(s_row_figures, 1)

            def edge_scores(l, plan, tile, _):
                c, t = tile.cls, tile.t
                e = edge[tile.par][:, 0:c.chunks, 0:4]
                of_row = spread[tile.par][:, 0:8 * c.chunks].rearrange("p (c k) -> p c k", k=8)
                dve.wait_ge(s_spread, t)
                nc.vector.tensor_tensor(e, of_row[:, :, 0:4], rows_of(tile)[:, :, F:F + 4], ALU.add).then_inc(s_edge_step, 1)
                dve.wait_ge(s_edge_step, t * 3 - 2)
                nc.vector.scalar_tensor_tensor(e, e, ALPHA[l], e, ALU.mult, ALU.max).then_inc(s_edge_step, 1)
                dve.wait_ge(s_edge_step, t * 3 - 1)
                nc.vector.tensor_tensor(e, e, of_row[:, :, 4:8], ALU.add).then_inc(s_edge_step, 1)
                dve.wait_ge(s_edge_step, t * 3)
                nc.vector.tensor_scalar(e, e, 0.0, None, ALU.min).then_inc(s_edge, 1)

            def weigh(l, plan, tile, _):
                c, nh = tile.cls, HEADS[l]
                rows = rows_of(tile)
                by_head = rows[:, :, 0:F].rearrange("p c (h d) -> p c h d", h=nh)
                weights = rows[:, :, F:F + nh].unsqueeze(3).broadcast_to([P, c.chunks, nh, F // nh])
                dve.wait_ge(s_edge_exp, tile.t)
                nc.vector.tensor_tensor(by_head, by_head, weights, ALU.mult).then_inc(s_weighted, 1)

            def front_beside_combine(l, new, old):
                first_steps, last_steps = iter(()), iter(())
                if old:
                    last_steps = combine(l, SPARSE, old[0], HEADS[l] - 1)
                if new:
                    first_steps = front_heads(l, SPARSE, *new) if HEADS[l] > 1 else front(l, SPARSE, *new)
                for _ in first_steps:
                    next(last_steps, None)
                for _ in last_steps:
                    pass

            def elu_tile(l, plan, tile, _):
                elu(l, plan, tile, HEADS[l] - 1)

            def leaky_group(l, plan, tile, h, g):
                buf = scores[:, g * 512:(g + 1) * 512]
                if g < tile.cls.groups - 1:
                    dve.wait_ge(s_scored_part, dense_unit(l, plan, tile, h) * (TILES // BANK - 1) + (g + 1))
                else:
                    dve.wait_ge(s_scored, unit_index(l, tile, h) + 1)
                op = nc.vector.scalar_tensor_tensor(buf, buf, ALPHA[l], buf, ALU.mult, ALU.max)
                op.then_inc(s_leaky_part if g < tile.cls.groups - 1 else s_leaky, 1)

            def dense_tile(l, plan, tile):
                last = HEADS[l] - 1
                for h in range(HEADS[l]):
                    for _ in front(l, plan, tile, h):
                        pass
                    leaky_group(l, plan, tile, h, tile.cls.groups - 1)
                threshold(l, plan, tile, last)
                for _ in combine(l, plan, tile, last):
                    pass
                elu(l, plan, tile, last)

            def leaky_relu(l, plan, tile, h):
                c, u, t, p = tile.cls, unit_index(l, tile, h), tile.t, tile_slot(tile)
                wide = c.chunks * P
                buf = attn_buffer(l, tile, h)
                dve.wait_ge(s_scored, u + 1)
                nc.vector.scalar_tensor_tensor(buf[:, 0:wide], buf[:, 0:wide], ALPHA[l], buf[:, 0:wide],
                                               ALU.mult, ALU.max).then_inc(s_leaky, 1)

            def threshold(l, plan, tile, h):
                if l != 2:
                    return
                t, p = tile.t, tile_slot(tile)
                buf = attn_buffer(l, tile, h)[:, 0:tile.cls.chunks * P]
                dve.wait_ge(s_exped, unit_index(l, tile, h) + 1)
                nc.vector.tensor_scalar(st[:, p, LEAST, 0:1], st[:, p, SUM, 0:1], THRESHOLD, None, ALU.mult)\
                    .then_inc(s_attn, 1)
                dve.wait_ge(s_attn, t + 1)
                nc.vector.scalar_tensor_tensor(buf, buf, st[:, p, LEAST, 0:1], buf, ALU.is_ge, ALU.mult)\
                    .then_inc(s_normed, 1)

            def combine(l, plan, tile, h):
                nh = HEADS[l]
                if h < nh - 1:
                    return
                c, u, t = tile.cls, unit_index(l, tile, h), tile.t
                p, n = tile_slot(tile), tile.t + l * TILES
                slotwise = nh > 1 and not c.dense
                if not slotwise:
                    dve.wait_ge(s_exped, u + 1)
                    if c.dense and l != 2:
                        nc.vector.tensor_reduce(st[:, p, SUM, 0:nh], group_max[:, 3, 0:4 * nh].rearrange("p (h i) -> p h i", i=4),
                                                AX, ALU.add).then_inc(s_dense_sum, 1)
                        dve.wait_ge(s_dense_sum, dense_sums(l, plan, tile) + 1)
                    nc.vector.reciprocal(st[:, p, RSUM, 0:nh], st[:, p, SUM, 0:nh]).then_inc(s_recip, 1)
                nc.vector.tensor_scalar(st[:, p, VALID, 0:nh], st[:, p, BIGGEST, 0:nh], LOW, None, ALU.is_gt)
                nc.vector.tensor_scalar(st[:, p, EMPTY, 0:nh], st[:, p, BIGGEST, 0:nh], LOW, None, ALU.is_le)\
                    .then_inc(s_scale, 1)
                yield
                dve.wait_ge(s_scale, n * 2 + 1)
                if slotwise:
                    dve.wait_ge(s_summed, t)
                    nc.vector.tensor_tensor(st[:, p, SUM, 0:nh], AG[tile.par][:, F:F + nh], st[:, p, EMPTY, 0:nh], ALU.add)\
                        .then_inc(s_sum_kept, 1)
                    yield
                    dve.wait_ge(s_sum_kept, t)
                    nc.vector.reciprocal(st[:, p, RSUM, 0:nh], st[:, p, SUM, 0:nh]).then_inc(s_recip, 1)
                    yield
                dve.wait_ge(s_recip, n + 1)
                if l == 2:
                    pieces, wide = count_pieces(tile), c.chunks * P
                    nc.vector.tensor_reduce(st[:, p, VALIDS, 0:1], st[:, p, COUNT, 0:pieces], AX, ALU.add).then_inc(s_counted, 1)
                    yield
                    dve.wait_ge(s_counted, 2 * t + 1)
                    nc.vector.tensor_scalar(st[:, p, VALIDS, 0:1], st[:, p, VALIDS, 0:1], float(wide), 0.5, ALU.add, ALU.mult)\
                        .then_inc(s_counted, 1)
                    yield
                    dve.wait_ge(s_counted, 2 * t + 2)
                    nc.vector.scalar_tensor_tensor(st[:, p, KEEP, 0:1], st[:, p, RSUM, 0:1], THRESHOLD,
                                                   st[:, p, VALIDS, 0:1], ALU.is_gt, ALU.mult).then_inc(s_fin_a, 1)
                    yield
                    dve.wait_ge(s_fin_a, t + 1)
                    nc.vector.scalar_tensor_tensor(st[:, p, SCALE, 0:1], st[:, p, VALID, 0:1], st[:, p, RSUM, 0:1],
                                                   st[:, p, KEEP, 0:1], ALU.mult, ALU.mult)\
                        .then_inc(s_scale, 1)
                else:
                    nc.vector.tensor_tensor(st[:, p, SCALE, 0:nh], st[:, p, VALID, 0:nh], st[:, p, RSUM, 0:nh], ALU.mult)\
                        .then_inc(s_scale, 1)
                yield
                dve.wait_ge(s_scale, n * 2 + 2)
                if not slotwise:
                    dve.wait_ge(s_agg_group, group_index(l, plan, tile, h, c.groups - 1) + 1)
                if due(n):
                    dve.wait_ge(s_x_done, n)
                ag, xt = AG[tile_parity(tile)][:, 0:F], xs[:, t, :]
                scale, empty = st[:, p, SCALE, 0:nh], st[:, p, EMPTY, 0:nh]
                if l < 2:
                    nc.vector.scalar_tensor_tensor(y[:, :], ag, scale, xt, ALU.mult, ALU.add).then_inc(s_fin_b, 1)
                    yield
                    dve.wait_ge(s_fin_b, n + 1)
                    nc.vector.scalar_tensor_tensor(xt, hbar[:, :], empty, y[:, :], ALU.mult, ALU.add)\
                        .then_inc(s_x_done, 1)
                    return
                m = t + (l - 2) * TILES
                if l == 2:
                    nc.vector.scalar_tensor_tensor(y[:, :], ag, scale, hs[:, t, 0:F], ALU.mult, ALU.add)\
                        .then_inc(s_fin_y, 1)
                else:
                    by_head = ag.rearrange("p (h d) -> p h d", h=nh)
                    hb = hbar[:, :].rearrange("p (h d) -> p h d", h=nh)
                    y3, y23 = (a[:, :].rearrange("p (h d) -> p h d", h=nh) for a in (y, y2))
                    nc.vector.tensor_tensor(y3, by_head, scale.unsqueeze(2).broadcast_to([P, nh, F // nh]), ALU.mult)
                    nc.vector.tensor_tensor(y23, hb, empty.unsqueeze(2).broadcast_to([P, nh, F // nh]), ALU.mult)\
                        .then_inc(s_fin_b, 1)
                    yield
                    dve.wait_ge(s_fin_b, t + (2 * TILES + 1))
                    nc.vector.tensor_tensor(y[:, :], y[:, :], y2[:, :], ALU.add).then_inc(s_fin_y, 1)
                yield
                dve.wait_ge(s_fin_y, m + 1)
                nc.vector.tensor_scalar(neg[:, :], y[:, :], 0.0, None, ALU.min).then_inc(s_neg, 1)

            def elu(l, plan, tile, h):
                if l < 2 or h < HEADS[l] - 1:
                    return
                m, xt = tile.t + (l - 2) * TILES, xs[:, tile.t, :]
                dve.wait_ge(s_exp_neg, m + 1)
                nc.vector.scalar_tensor_tensor(y2[:, :], y[:, :], 0.0, exp_neg[:, :], ALU.max, ALU.add)\
                    .then_inc(s_elu, 1)
                dve.wait_ge(s_elu, m + 1)
                nc.vector.scalar_tensor_tensor(xt, y2[:, :], -1.0, xt, ALU.add, ALU.add).then_inc(s_x_done, 1)

            dve.wait_ge(s_flag, 1)
            many = dve.value_load(over_int[0:1, 0:1])
            with dve.If(many < 1):
                for l in range(LAYERS):
                    if HEADS[l] > 1:
                        stages = [((0, 3), front_beside_combine), (1, edge_scores), (3, elu_tile), (1, weigh)]
                    else:
                        stages = [(0, mask_slots), (1, threshold), ((0, 2), front_beside_combine),
                                  (0, leaky_relu), (2, elu)]
                    node_work = [(2, 1, node_stats), (3, 2, node_keep), (3, 1, node_normal)]

                    def quad_work(tiles, quad, back_tiles):
                        if tiles[0].cls.dense:
                            dense_tile(l, SPARSE, tiles.pop(0))
                            if HEADS[l] > 1:
                                dve.wait_ge(s_x_done, l * TILES + 1)
                        run_quad(l, stages, node_parts(dve, l + 1, node_work), tiles, back_tiles, quad)
                    last = over_plan(dve, SPARSE, quad_work)
                    run_rest(l, stages, last)
                    if l < 3:
                        node_keep(dve, l + 1, TILES // 4 - 2)
                        node_stats(dve, l + 1, TILES // 4 - 1)
                        node_normal(dve, l + 1, TILES // 4 - 1)
                        node_keep(dve, l + 1, TILES // 4 - 1)
                        mean_begin(dve, l + 1)
                        mean_keep(dve, l + 1)
                dve.nop()
            with dve.Else():
                for l in range(LAYERS):
                    over_plan(dve, DENSE, lambda tiles, quad, back: dense_tile(l, DENSE, tiles[0]))
                    if l < 3:
                        def node_all(quad):
                            node_stats(dve, l + 1, quad)
                            node_normal(dve, l + 1, quad)
                            node_keep(dve, l + 1, quad)
                        over_quads(dve, node_all)
                        mean_begin(dve, l + 1)
                        mean_keep(dve, l + 1)
                dve.nop()


_INS = ["x", "adj", "L0_gnn_W", "L0_gnn_a", "L1_gnn_W", "L1_gnn_a", "L2_gnn_W", "L2_gnn_a", "L3_gnn_W", "L3_gnn_a"]


def kernel(**inputs):
    import numpy as _np
    import concourse.bacc as _bacc
    from concourse import mybir as _mybir
    from concourse.bass_utils import run_bass_kernel_spmd as _run

    nc = _bacc.Bacc("TRN2", target_bir_lowering=False, num_devices=1)
    arrays, args = {}, []
    for name in _INS:
        a = _np.ascontiguousarray(inputs[name])
        arrays[f"in_{name}"] = a
        args.append(nc.dram_tensor(f"in_{name}", a.shape, _mybir.dt.from_np(a.dtype), kind="ExternalInput").ap())
    args.append(nc.dram_tensor("out_x", (8192, 128), _mybir.dt.float32, kind="ExternalOutput").ap())
    gat_kernel(nc, *args)
    r = _run(nc, [arrays], core_ids=[0])
    return r.results[0]["out_x"]
```
